# Optimizing a Trainium2 kernel written in Bass

```python
import numpy as np
import jax
import jax.numpy as jnp

def _softmax(x, axis=-1):
    return jax.nn.softmax(x, axis=axis)
def _gelu(x):
    return jax.nn.gelu(x, approximate=True)
def _silu(x):
    return jax.nn.silu(x)
def _sigmoid(x):
    return jax.nn.sigmoid(x)
def _layernorm(x, axis=-1, eps=1e-5):
    m = jnp.mean(x, axis=axis, keepdims=True)
    v = jnp.var(x, axis=axis, keepdims=True)
    return (x - m) / jnp.sqrt(v + eps)
def _scatter_add(tgt, idx, src, axis=0):
    return tgt.at[idx].add(src)
def _segment_sum(src, seg, n):
    return jax.ops.segment_sum(src, seg, n)

kernel_name = 'mk_metaformer_d1_conv_nchw128_057886'

def setup_inputs(seed: int = 0):
    np.random.seed(seed)
    _w = jnp.asarray
    def _rec_inputs():
        import jax
        import jax.numpy as jnp
        _gk = jax.random.key(seed)
        x = 7.22e-05 + 1 * jax.random.normal(jax.random.fold_in(_gk, 1), (4, 128, 128, 128), jnp.float32)
        return x
    x = _rec_inputs()
    def _L0_conv_setup():
        import jax, jax.numpy as jnp
        import numpy as np
        DIM = 128
        HID = 4 * DIM
        EPS = 1e-05

        def _ln(x, g, b):
            mu = jnp.mean(x, axis=-1, keepdims=True)
            var = jnp.mean(jnp.square(x - mu), axis=-1, keepdims=True)
            return (x - mu) * jax.lax.rsqrt(var + EPS) * g + b

        def _block(x, ln0_g, ln0_b, ln1_g, ln1_b, ln2_g, ln2_b, W_out, W_whiten, W_key, W_recep, W_value):
            b, c, h, w = x.shape
            t = x.reshape(b, c, h * w).transpose(0, 2, 1)
            t = _ln(t, ln0_g, ln0_b)
            y1 = _ln(t, ln1_g, ln1_b)
            att = jnp.einsum('btc,oc->bto', jax.nn.sigmoid(y1) * y1, W_out)
            t = t + att
            y2 = _ln(t, ln2_g, ln2_b)
            wht = jnp.einsum('btc,oc->bto', y2, W_whiten)
            k = jnp.square(jax.nn.relu(jnp.einsum('btc,hc->bth', wht, W_key)))
            kv = jnp.einsum('bth,ch->btc', k, W_value)
            r = jax.nn.sigmoid(jnp.einsum('btc,oc->bto', wht, W_recep))
            t = t + r * kv
            return t.transpose(0, 2, 1).reshape(b, c, h, w)
        key = jax.random.key(seed)
        ks = jax.random.split(key, 8)
        b, c, h, w = (4, DIM, 128, 128)
        inp = {'inp_img': jax.random.normal(ks[0], (b, c, h, w), dtype=jnp.float32), 'ln0_g': jnp.ones((c,), jnp.float32), 'ln0_b': jnp.zeros((c,), jnp.float32), 'ln1_g': jnp.ones((c,), jnp.float32), 'ln1_b': jnp.zeros((c,), jnp.float32), 'ln2_g': jnp.ones((c,), jnp.float32), 'ln2_b': jnp.zeros((c,), jnp.float32), 'W_out': jax.random.normal(ks[1], (c, c), jnp.float32) * 0.05, 'W_whiten': jax.random.normal(ks[2], (c, c), jnp.float32) * 0.05, 'W_key': jax.random.normal(ks[3], (HID, c), jnp.float32) * 0.05, 'W_recep': jax.random.normal(ks[4], (c, c), jnp.float32) * 0.05, 'W_value': jax.random.normal(ks[5], (c, HID), jnp.float32) * 0.05}
        return inp
    _L0_conv_all = _L0_conv_setup()
    _L0_conv_in = {k: v for k, v in _L0_conv_all.items() if k in ('ln0_g', 'ln0_b', 'ln1_g', 'ln1_b', 'ln2_g', 'ln2_b', 'W_out', 'W_whiten', 'W_key', 'W_recep', 'W_value', )}
    del _L0_conv_all

    def _L0_ffn_setup():
        import jax, jax.numpy as jnp
        import numpy as np
        BN_EPS = 1e-05
        key = jax.random.key(seed)
        k1, k2, k3 = jax.random.split(key, 3)
        B, T, I, H = (64, 2048, 128, 128)
        x = jax.random.normal(k1, (B, T, I), dtype=jnp.float32)
        W = jax.random.normal(k2, (H, I), dtype=jnp.float32) * (1.0 / np.sqrt(I))
        V = jnp.linalg.qr(jax.random.normal(k3, (H, H), dtype=jnp.float32))[0]
        gamma = jnp.ones((H,), dtype=jnp.float32)
        beta = jnp.zeros((H,), dtype=jnp.float32)
        return {'x': x, 'W': W, 'V': V, 'gamma': gamma, 'beta': beta}
    _L0_ffn_all = _L0_ffn_setup()
    _L0_ffn_in = {k: v for k, v in _L0_ffn_all.items() if k in ('W', 'V', 'gamma', 'beta', )}
    del _L0_ffn_all

    return {
        "x": x,
        "L0_conv_ln0_g": _L0_conv_in["ln0_g"],
        "L0_conv_ln0_b": _L0_conv_in["ln0_b"],
        "L0_conv_ln1_g": _L0_conv_in["ln1_g"],
        "L0_conv_ln1_b": _L0_conv_in["ln1_b"],
        "L0_conv_ln2_g": _L0_conv_in["ln2_g"],
        "L0_conv_ln2_b": _L0_conv_in["ln2_b"],
        "L0_conv_W_out": _L0_conv_in["W_out"],
        "L0_conv_W_whiten": _L0_conv_in["W_whiten"],
        "L0_conv_W_key": _L0_conv_in["W_key"],
        "L0_conv_W_recep": _L0_conv_in["W_recep"],
        "L0_conv_W_value": _L0_conv_in["W_value"],
        "L0_ffn_W": _L0_ffn_in["W"],
        "L0_ffn_V": _L0_ffn_in["V"],
        "L0_ffn_gamma": _L0_ffn_in["gamma"],
        "L0_ffn_beta": _L0_ffn_in["beta"],
    }

def reference(x, L0_conv_ln0_g, L0_conv_ln0_b, L0_conv_ln1_g, L0_conv_ln1_b, L0_conv_ln2_g, L0_conv_ln2_b, L0_conv_W_out, L0_conv_W_whiten, L0_conv_W_key, L0_conv_W_recep, L0_conv_W_value, L0_ffn_W, L0_ffn_V, L0_ffn_gamma, L0_ffn_beta):
    import jax
    import jax.numpy as jnp
    def _L0_conv_ref(inp_img, ln0_g, ln0_b, ln1_g, ln1_b, ln2_g, ln2_b, W_out, W_whiten, W_key, W_recep, W_value):
        import jax, jax.numpy as jnp
        import numpy as np
        DIM = 128
        HID = 4 * DIM
        EPS = 1e-05

        def _ln(x, g, b):
            mu = jnp.mean(x, axis=-1, keepdims=True)
            var = jnp.mean(jnp.square(x - mu), axis=-1, keepdims=True)
            return (x - mu) * jax.lax.rsqrt(var + EPS) * g + b

        def _block(x, ln0_g, ln0_b, ln1_g, ln1_b, ln2_g, ln2_b, W_out, W_whiten, W_key, W_recep, W_value):
            b, c, h, w = x.shape
            t = x.reshape(b, c, h * w).transpose(0, 2, 1)
            t = _ln(t, ln0_g, ln0_b)
            y1 = _ln(t, ln1_g, ln1_b)
            att = jnp.einsum('btc,oc->bto', jax.nn.sigmoid(y1) * y1, W_out)
            t = t + att
            y2 = _ln(t, ln2_g, ln2_b)
            wht = jnp.einsum('btc,oc->bto', y2, W_whiten)
            k = jnp.square(jax.nn.relu(jnp.einsum('btc,hc->bth', wht, W_key)))
            kv = jnp.einsum('bth,ch->btc', k, W_value)
            r = jax.nn.sigmoid(jnp.einsum('btc,oc->bto', wht, W_recep))
            t = t + r * kv
            return t.transpose(0, 2, 1).reshape(b, c, h, w)
        params = (ln0_g, ln0_b, ln1_g, ln1_b, ln2_g, ln2_b, W_out, W_whiten, W_key, W_recep, W_value)
        out1 = _block(inp_img, *params)
        out2 = _block(inp_img.transpose(0, 1, 3, 2), *params).transpose(0, 1, 3, 2)
        return out2 + out1

    def _L0_ffn_ref(x, W, V, gamma, beta):
        import jax, jax.numpy as jnp
        import numpy as np
        BN_EPS = 1e-05
        B, T, H = (x.shape[0], x.shape[1], W.shape[0])
        Wx = jnp.einsum('bti,hi->bth', x, W)
        flat = Wx.reshape(B * T, H)
        mean = jnp.mean(flat, axis=0)
        var = jnp.var(flat, axis=0)
        Wx = ((flat - mean) * jax.lax.rsqrt(var + BN_EPS) * gamma + beta).reshape(B, T, H)
        Vt = V.T

        def step(yt, wx_t):
            yt = jax.nn.sigmoid(wx_t + yt @ Vt)
            return (yt, yt)
        y0 = jnp.zeros((B, H), dtype=Wx.dtype)
        _, ys = jax.lax.scan(step, y0, jnp.swapaxes(Wx, 0, 1))
        return jnp.swapaxes(ys, 0, 1)

    def _gn(v, G=32, eps=1e-5):
        B_, C_, H_, W_ = v.shape
        g = v.reshape(B_, G, C_ // G, H_, W_)
        m = jnp.mean(g, axis=(2, 3, 4), keepdims=True)
        s = jnp.var(g, axis=(2, 3, 4), keepdims=True)
        return ((g - m) / jnp.sqrt(s + eps)).reshape(v.shape)

    def _ln_c(v, eps=1e-6):
        m = jnp.mean(v, axis=1, keepdims=True)
        s = jnp.var(v, axis=1, keepdims=True)
        return (v - m) / jnp.sqrt(s + eps)

    def _ln_t(v, eps=1e-5):
        m = jnp.mean(v, axis=-1, keepdims=True)
        s = jnp.var(v, axis=-1, keepdims=True)
        return (v - m) / jnp.sqrt(s + eps)

    def _to_tokens(v):
        B_, C_, H_, W_ = v.shape
        return v.reshape(B_, C_, H_ * W_).transpose(0, 2, 1)
    def _from_tokens(t, like):
        B_, C_, H_, W_ = like.shape
        return t.transpose(0, 2, 1).reshape(B_, C_, H_, W_)

    x = x + _L0_conv_ref(_ln_c(x), L0_conv_ln0_g, L0_conv_ln0_b, L0_conv_ln1_g, L0_conv_ln1_b, L0_conv_ln2_g, L0_conv_ln2_b, L0_conv_W_out, L0_conv_W_whiten, L0_conv_W_key, L0_conv_W_recep, L0_conv_W_value)
    t = _to_tokens(x)
    t = t + _L0_ffn_ref(_ln_t(t), L0_ffn_W, L0_ffn_V, L0_ffn_gamma, L0_ffn_beta)
    x = _from_tokens(t, x)
    return x


_drawn_inputs = setup_inputs


def setup_inputs(seed=0):
    import zlib

    import numpy as np

    out = dict(_drawn_inputs(seed))
    spreads = {'L0_conv_ln0_g': (1.0, 0.2),
     'L0_conv_ln0_b': (0.0, 0.1),
     'L0_conv_ln1_g': (1.0, 0.2),
     'L0_conv_ln1_b': (0.0, 0.412),
     'L0_conv_ln2_g': (1.0, 0.6),
     'L0_conv_ln2_b': (0.0, 0.8),
     'L0_ffn_gamma': (1.0, 0.6),
     'L0_ffn_beta': (0.0, 0.8)}
    factors = {'L0_conv_W_recep': 7.072}
    for name, (base, spread) in spreads.items():
        noise = np.random.default_rng([zlib.crc32(name.encode()), seed]).standard_normal(out[name].shape)
        drawn = base * np.exp(spread * noise) if base else spread * noise
        out[name] = jnp.asarray(drawn.astype(out[name].dtype))
    for name, factor in factors.items():
        out[name] = (out[name] * factor).astype(out[name].dtype)
    return out
```

```python
import concourse.bass as bass
from concourse import mybir
from contextlib import ExitStack


def metaformer_kernel(nc, x, ln0_g, ln0_b, ln1_g, ln1_b, ln2_g, ln2_b,
                      W_out, W_whiten, W_key, W_recep, W_value,
                      W_ffn, V_ffn, bn_gamma, bn_beta, out):
    f32, f32r, i32 = mybir.dt.float32, mybir.dt.float32r, mybir.dt.int32
    ALU, ACT, AX = mybir.AluOpType, mybir.ActivationFunctionType, mybir.AxisListType

    B, C, H, Wd = x.shape
    T = H * Wd
    N = 512
    NT = B * T // N
    TPB = T // N
    HB = W_key.shape[0] // C
    L = 32
    CPT = N // L
    NC = T // L
    WARM = 14
    TOL = 2.0 ** -21
    G = 2
    GC = NC // G
    GT = TPB // G
    LN_EPS = 1e-5
    KAPPA = (1.0 + LN_EPS) ** -0.5
    EPS0 = LN_EPS * 1e-6 / (1.0 + LN_EPS)

    x_d = x.rearrange("b c h w -> b c (h w)")
    out_d = out.rearrange("b c h w -> b c (h w)")
    xp_d = nc.dram_tensor("x_prime", (C, NT * N), f32, kind="Internal").ap()
    wx_d = nc.dram_tensor("w_x", (C, NT * N), f32, kind="Internal").ap()

    ctx = ExitStack()
    with ctx:
        def sb(name, cols, dt=f32, rows=C):
            return ctx.enter_context(nc.sbuf_tensor(name, [rows, cols], dt))

        def sem(name):
            return ctx.enter_context(nc.semaphore(name))

        def sems(name, n):
            return [sem(f"{name}{i}") for i in range(n)]

        ident = sb("ident", C)
        center = sb("center", C)
        center_r = sb("center_r", C, f32r)
        mean_w = sb("mean_w", C)
        neg_half = sb("neg_half", N)
        vecs = sb("vecs", 8)
        g0, b0, g1, b1, g2, b2, gamma, beta = (vecs[:, k:k + 1] for k in range(8))
        kg0 = sb("kg0", 1)
        pb0 = sb("pb0", 1)
        hid_bias = sb("hid_bias", HB + 1)
        m1_hi, m1_lo = sb("m1_hi", C, f32r), sb("m1_lo", C, f32r)
        key_hi, key_lo = sb("key_hi", HB * C, f32r), sb("key_lo", HB * C, f32r)
        rec_hi, rec_lo = sb("rec_hi", C, f32r), sb("rec_lo", C, f32r)
        wf_hi, wf_lo = sb("wf_hi", C, f32r), sb("wf_lo", C, f32r)
        value_T = sb("value_T", HB * C)
        small_T = sb("small_T", 4 * C)
        out_T, rec_T, ffn_T, V_T = (small_T[:, k * C:(k + 1) * C] for k in range(4))

        x_hi, x_lo = sb("x_hi", N, f32r), sb("x_lo", N, f32r)
        t1_hi, t1_lo = sb("t1_hi", N, f32r), sb("t1_lo", N, f32r)
        y2_hi, y2_lo = sb("y2_hi", N, f32r), sb("y2_lo", N, f32r)
        xp_hi, xp_lo = sb("xp_hi", N, f32r), sb("xp_lo", N, f32r)

        wx_even = sb("wx_even", T)
        arena = sb("arena", 44 * N)
        wx_buf = [wx_even[:, :], arena[:, 0:T]]
        arena_at = [0]

        def tile(n=1):
            at = arena_at[0]
            arena_at[0] += n
            return [arena[:, (at + k) * N:(at + k + 1) * N] for k in range(n)]

        x_in = tile(4)
        (sq0,), (sq1,), (sq2,), (sqe,) = (tile() for _ in range(4))
        (v0,), (v1,), (v2,), (ve,) = (tile() for _ in range(4))
        (rs0,), (rs1,), (rs2,), (rse,) = (tile() for _ in range(4))
        (t0c,), (t0p,), (u1,), (sg,), (y1,), (gate,), (y2,) = (tile() for _ in range(7))
        t1 = tile(2)
        relu = tile(HB)
        hid = tile(HB)
        recep = tile(2)
        (rkv,), (t2,) = tile(), tile()
        xp = tile(2)
        wx = tile(2)
        assert arena_at[0] <= 44

        stage = arena[:, T:T + 3 * 4 * N]
        bn_parts = sb("bn_parts", NT * 6)
        bn_mv = sb("bn_mv", 2)
        bn_small = sb("bn_small", 3)
        bn_scale = sb("bn_scale", 1)
        bn_bias = sb("bn_bias", 1)
        warm_y = sb("warm_y", NC)
        start_y = sb("start_y", NC)
        pre = sb("pre", NC)
        diff = pre
        agree = sb("agree", B)
        agree_all = sb("agree_all", 1)
        agree_f = sb("agree_f", 1, rows=1)
        agree_i = sb("agree_i", 1, i32, rows=1)

        banks = [ctx.enter_context(nc.psum_tensor(f"bank{k}", [C, N], f32)) for k in range(8)]
        p_xc, p_m1, p_var, p_t, p_ha, p_hb, p_kv, p_x = banks

        weights_in, pool_prep, dve_prep, pe_prep = (sem(n) for n in ("weights_in", "pool_prep", "dve_prep", "pe_prep"))
        x_loaded = sems("x_loaded", 4)
        xp_stored = sems("xp_stored", 2)
        wx_stored = sems("wx_stored", 2)
        x_hi_ok, t1_ok, t1_hi_ok, t1_lo_ok, t0c_ok, t0p_ok, y2_ok, y2_hi_ok, y2_lo_ok = (
            sem(n) for n in ("x_hi_ok", "t1_ok", "t1_hi_ok", "t1_lo_ok", "t0c_ok", "t0p_ok", "y2_ok", "y2_hi_ok", "y2_lo_ok"))
        wx_ok, bn_ok, u1_ok, y1_ok, gate_ok, rkv_ok, xp_ok, xp_hi_ok, k_dve = (
            sem(n) for n in ("wx_ok", "bn_ok", "u1_ok", "y1_ok", "gate_ok", "rkv_ok", "xp_ok", "xp_hi_ok", "k_dve"))
        x_lo_ok, rs0_ok, rs1_ok, rs2_ok, rse_ok, t2_ok, xp_lo_ok = (
            sem(n) for n in ("x_lo_ok", "rs0_ok", "rs1_ok", "rs2_ok", "rse_ok", "t2_ok", "xp_lo_ok"))
        sq0_ok, sq1_ok, sq2_ok, sqe_ok, v0_ok, v1_ok, v2_ok, ve_ok = (
            sem(n) for n in ("sq0_ok", "sq1_ok", "sq2_ok", "sqe_ok", "v0_ok", "v1_ok", "v2_ok", "ve_ok"))
        sg_ok, recep_ok, relu_ok, k_act = (sem(n) for n in ("sg_ok", "recep_ok", "relu_ok", "k_act"))
        xc_mm, m1_mm, v0_mm, v1_mm, v2_mm, ve_mm, att_mm, t1c_mm = (
            sem(n) for n in ("xc_mm", "m1_mm", "v0_mm", "v1_mm", "v2_mm", "ve_mm", "att_mm", "t1c_mm"))
        rec_mm, hid_mm, kva_mm, kv_mm, xpc_mm, wx_mm = (
            sem(n) for n in ("rec_mm", "hid_mm", "kva_mm", "kv_mm", "xpc_mm", "wx_mm"))
        bn_dve, bn_pool, bn_ready = sem("bn_dve"), sem("bn_pool"), sem("bn_ready")
        wx_back = sems("wx_back", 2)
        stage_in = sems("stage_in", 3)
        stage_out = sems("stage_out", 3)
        z_mm, pre_ok, y_ok = sems("z_mm", G), sems("pre_ok", G), sems("y_ok", G)
        start_ok, added, checked, checked_part, flag_mm, flag_part, flag_ok = (
            sem(n) for n in ("start_ok", "added", "checked", "checked_part", "flag_mm", "flag_part", "flag_ok"))
        seq_in, seq_out, seq_free, seq_z, seq_pre, seq_y, seq_add, seq_zero = (
            sem(n) for n in ("seq_in", "seq_out", "seq_free", "seq_z", "seq_pre", "seq_y", "seq_add", "seq_zero"))

        PREP_DMAS = 8 + 7

        FIRST, LAST = -1, NT + 2
        LOOP = (4, NT - 4)
        PER_LOOP = range(3, 7)

        def phase1(eng, step):
            for i in range(FIRST, LOOP[0] + PER_LOOP[0]):
                step(0, i)
            with eng.Fori(LOOP[0], LOOP[1] - 3, 4) as base:
                for m in PER_LOOP:
                    step(base, m)
            for i in range(LOOP[1] + PER_LOOP[0], LAST + 1):
                step(0, i)

        def live(base, n):
            return not isinstance(base, int) or 0 <= base + n < NT

        def wait(eng, s, count):
            if not isinstance(count, int) or count > 0:
                eng.wait_ge(s, count)

        def ring(base, m, size, each=16):
            return base * (each // size) + each * (m // size + 1)

        seq_wx = wx_even[:, 0:B * N].rearrange("c (b n) -> c b n", b=B)
        seq_xp = wx_even[:, B * N:2 * B * N].rearrange("c (b n) -> c b n", b=B)
        seq_y_buf = start_y[:, 0:B]
        seq_pre_buf = pre[:, 0:B]

        def by_step(buf):
            return buf.rearrange("p (t s c) -> p t s c", s=L, c=CPT)

        def group_of(buf, g, s):
            return by_step(buf)[:, g * GT:(g + 1) * GT, bass.ds(s, 1), :].rearrange("p t s c -> p (t s) c")

        def cols(ap):
            return ap.rearrange("p (t c) -> p t c", c=CPT)

        block = ctx.enter_context(nc.Block())

        @block.sync
        def _(sp):
            for k, v in enumerate((ln0_g, ln0_b, ln1_g, ln1_b, ln2_g, ln2_b, bn_gamma, bn_beta)):
                sp.dma_start(vecs[:, k:k + 1], v.rearrange("(c o) -> c o", o=1)).then_inc(weights_in, 16)
            sp.dma_start(hid[0][:, :].rearrange("p (j c) -> p j c", c=C),
                         W_key.rearrange("(j p) c -> p j c", p=C)).then_inc(weights_in, 16)
            sp.dma_start(hid[1][:, :], W_value).then_inc(weights_in, 16)
            for k, w in enumerate((W_out, W_recep, W_ffn, V_ffn)):
                sp.dma_start(hid[2][:, k * C:(k + 1) * C], w).then_inc(weights_in, 16)
            sp.dma_start(hid[3][:, 0:C], W_whiten).then_inc(weights_in, 16)

            def load_and_store(b, base, m):
                if live(base, m - 4):
                    wait(sp, xp_ok, base + m - 3)
                if live(base, m):
                    col = (base + m - b * TPB) * N
                    sp.dma_start(x_in[m % 4], x_d[b, :, bass.ds(col, N)]).then_inc(x_loaded[m % 4], 16)
                if live(base, m - 4):
                    sp.dma_start(xp_d[:, bass.ds((base + m - 4) * N, N)], xp[m % 2]).then_inc(xp_stored[m % 2], 16)
                if live(base, m - 5):
                    wait(sp, wx_ok, base + m - 4)
                    sp.dma_start(wx_d[:, bass.ds((base + m - 5) * N, N)], wx[(m - 5) % 2])\
                      .then_inc(wx_stored[(m - 5) % 2], 16)

            for m in range(8):
                load_and_store(0, 0, m)
            for b in range(B):
                if b == 2:
                    for s in wx_stored:
                        sp.wait_ge(s, 16 * TPB // 2)
                    sp.dma_start(wx_buf[0], wx_d[:, 0:T]).then_inc(wx_back[0], 16)
                with sp.Fori(max(b * TPB, 8), (b + 1) * TPB - 3, 4) as base:
                    for m in range(4):
                        load_and_store(b, base, m)
            for m in range(NT, NT + 5):
                load_and_store(B - 1, 0, m)

            for s in xp_stored + wx_stored:
                sp.wait_ge(s, 16 * NT // 2)
            sp.wait_ge(bn_ok, NT)
            sp.dma_start(wx_buf[1], wx_d[:, T:2 * T]).then_inc(wx_back[1], 16)
            SW = 4 * N
            NS = NT // 4

            def stage_load(k):
                if k >= 3:
                    sp.wait_ge(stage_out[k % 3], 16 * (k // 3))
                sp.dma_start(stage[:, (k % 3) * SW:(k % 3 + 1) * SW], xp_d[:, k * SW:(k + 1) * SW])\
                  .then_inc(stage_in[k % 3], 16)

            stage_load(0)
            stage_load(1)
            for k in range(NS):
                if k + 2 < NS:
                    stage_load(k + 2)
                sp.wait_ge(added, 4 * (k + 1))
                b, col = k // (TPB // 4), k % (TPB // 4) * SW
                sp.dma_start(out_d[b, :, col:col + SW], stage[:, (k % 3) * SW:(k % 3 + 1) * SW])\
                  .then_inc(stage_out[k % 3], 16)
                if (k + 1) % (TPB // 4) == 0 and b + 2 < B:
                    sp.wait_ge(checked, b + 1)
                    sp.dma_start(wx_buf[b % 2], wx_d[:, (b + 2) * T:(b + 3) * T]).then_inc(wx_back[b % 2], 16)
            for s in range(3):
                sp.wait_ge(stage_out[s], 16 * ((NS - 1 - s) // 3 + 1))

            sp.wait_ge(flag_ok, 1)
            ok = sp.alloc_register("sp_ok")
            sp.reg_load(ok, agree_i[0:1, 0:1])
            with sp.If_eq(ok, 0):
                with sp.Fori(0, TPB) as t:
                    for dst, src in ((seq_wx, wx_d), (seq_xp, xp_d)):
                        sp.dma_start(dst, src.rearrange("c (b n) -> c b n", b=B)[:, :, bass.ds(t * N, N)])\
                          .then_inc(seq_in, 16)
                    sp.wait_ge(seq_add, (t + 1) * N)
                    sp.dma_start(out_d.rearrange("b c n -> c b n")[:, :, bass.ds(t * N, N)], seq_xp)\
                      .then_inc(seq_out, 16)
                    sp.wait_ge(seq_out, (t + 1) * 16)
                    sp.sem_inc(seq_free, 1)
            with sp.Else():
                sp.nop()

        @block.tensor
        def _(pe):
            pe.wait_ge(weights_in, 16 * PREP_DMAS)
            pe.wait_ge(pool_prep, 3)
            for j in range(HB):
                pe.transpose(p_xc[:, j * C:(j + 1) * C], hid[0][:, j * C:(j + 1) * C], ident[:, :])
                pe.transpose(p_m1[:, j * C:(j + 1) * C], hid[1][:, j * C:(j + 1) * C], ident[:, :])
                mm = pe.transpose(p_var[:, j * C:(j + 1) * C], hid[2][:, j * C:(j + 1) * C], ident[:, :])
            mm.then_inc(pe_prep, 1)
            pe.wait_ge(dve_prep, 7)
            pe.matmul(p_t[:, 0:C], center[:, :], sq1[:, 0:C], start=True, stop=True)
            pe.matmul(p_t[:, C:2 * C], center[:, :], ffn_T, start=True, stop=True)
            pe.matmul(p_t[:, 2 * C:2 * C + 1], center[:, :], b0, start=True, stop=True)
            pe.matmul(p_ha[:, :], hid[3][:, 0:C], sq0, start=True, stop=True)
            pe.matmul(p_hb[:, 0:C], hid[3][:, 0:C], rec_T, start=True, stop=True).then_inc(pe_prep, 1)
            pe.wait_ge(dve_prep, 9)
            for j in range(HB):
                pe.matmul(p_kv[:, j:j + 1], sq2[:, j * C:(j + 1) * C], b2, start=True, stop=True)
            pe.matmul(p_kv[:, HB:HB + 1], sqe[:, 0:C], b2, start=True, stop=True).then_inc(pe_prep, 1)
            pe.wait_ge(dve_prep, 20)

            def mm3(bank, hi, lo, m_hi, m_lo):
                pe.matmul(bank, lo, m_hi, start=True, stop=False)
                pe.matmul(bank, hi, m_lo, start=False, stop=False)
                return pe.matmul(bank, hi, m_hi, start=False, stop=True)

            def mm2(bank, m_hi, m_lo):
                pe.matmul(bank, center_r[:, :], m_lo, start=True, stop=False)
                return pe.matmul(bank, center_r[:, :], m_hi, start=False, stop=True)

            def step(base, m):
                n0, n1, n2, n3 = m, m - 1, m - 2, m - 3
                if live(base, n0):
                    wait(pe, x_hi_ok, base + n0 + 1)
                    wait(pe, x_lo_ok, base + n0 + 1)
                    wait(pe, t0p_ok, base + n0)
                    mm2(p_xc[:, :], x_hi[:, :], x_lo[:, :]).then_inc(xc_mm, 1)
                    wait(pe, t0c_ok, base + n0)
                    mm3(p_m1[:, :], m1_hi[:, :], m1_lo[:, :], x_hi[:, :], x_lo[:, :]).then_inc(m1_mm, 1)
                if live(base, n3):
                    wait(pe, xp_hi_ok, base + n3 + 1)
                    wait(pe, xp_lo_ok, base + n3 + 1)
                    wait(pe, wx_ok, base + n3)
                    mm2(p_x[:, :], xp_hi[:, :], xp_lo[:, :]).then_inc(xpc_mm, 1)
                if live(base, n0):
                    wait(pe, sq0_ok, base + n0 + 1)
                    wait(pe, v1_ok, base + n0)
                    pe.matmul(p_var[:, :], mean_w[:, :], sq0, start=True, stop=True).then_inc(v0_mm, 1)
                if live(base, n1):
                    wait(pe, t1_hi_ok, base + n1 + 1)
                    wait(pe, t1_lo_ok, base + n1 + 1)
                    mm2(p_t[:, :], t1_hi[:, :], t1_lo[:, :]).then_inc(t1c_mm, 1)
                if live(base, n3):
                    wait(pe, sqe_ok, base + n3 + 1)
                    if live(base, n0):
                        wait(pe, v0_ok, base + n0 + 1)
                    else:
                        wait(pe, v2_ok, base + n2 + 1 if live(base, n2) else NT)
                    pe.matmul(p_var[:, :], mean_w[:, :], sqe, start=True, stop=True).then_inc(ve_mm, 1)
                if live(base, n1):
                    wait(pe, sq2_ok, base + n1 + 1)
                    if live(base, n3):
                        wait(pe, ve_ok, base + n3 + 1)
                    elif live(base, n0):
                        wait(pe, v0_ok, base + n0 + 1)
                    pe.matmul(p_var[:, :], mean_w[:, :], sq2, start=True, stop=True).then_inc(v2_mm, 1)
                if live(base, n3):
                    mm3(p_x[:, :], wf_hi[:, :], wf_lo[:, :], xp_hi[:, :], xp_lo[:, :]).then_inc(wx_mm, 1)

                def value(first):
                    for j in range(2 * first, 2 * first + 2):
                        mm = pe.matmul(p_kv[:, :], value_T[:, j * C:(j + 1) * C], hid[j],
                                       start=(j == 0), stop=(j == HB - 1))
                    mm.then_inc(kv_mm if first else kva_mm, 1)

                if live(base, n2):
                    wait(pe, k_act, 2 * (base + n2) + 1)
                    wait(pe, k_dve, 2 * (base + n2) + 1)
                    wait(pe, rkv_ok, base + n2)
                    value(0)
                if live(base, n0):
                    wait(pe, sq1_ok, base + n0 + 1)
                    if live(base, n1):
                        wait(pe, v2_ok, base + n1 + 1)
                    else:
                        wait(pe, v0_ok, base + n0 + 1)
                    pe.matmul(p_var[:, :], mean_w[:, :], sq1, start=True, stop=True).then_inc(v1_mm, 1)
                if live(base, n2):
                    wait(pe, k_act, 2 * (base + n2) + 2)
                    wait(pe, k_dve, 2 * (base + n2) + 2)
                    value(1)
                if live(base, n1):
                    wait(pe, y2_hi_ok, base + n1 + 1)
                    wait(pe, y2_lo_ok, base + n1 + 1)
                    wait(pe, relu_ok, 4 * (base + n1))
                    mm3(p_ha[:, :], rec_hi[:, :], rec_lo[:, :], y2_hi[:, :], y2_lo[:, :]).then_inc(rec_mm, 1)
                    for j in range(HB):
                        if j == 1:
                            wait(pe, recep_ok, base + n1 + 1)
                        if j >= 2:
                            wait(pe, relu_ok, 4 * (base + n1) + j - 1)
                        mm3((p_hb, p_ha)[j % 2][:, :], key_hi[:, j * C:(j + 1) * C], key_lo[:, j * C:(j + 1) * C],
                            y2_hi[:, :], y2_lo[:, :]).then_inc(hid_mm, 1)
                if live(base, n0):
                    wait(pe, gate_ok, base + n0 + 1)
                    wait(pe, y2_ok, base + n0)
                    wait(pe, sq2_ok, base + n0)
                    pe.matmul(p_t[:, :], out_T, gate, start=True, stop=True).then_inc(att_mm, 1)

            phase1(pe, step)

            def v_y(g, y):
                pe.matmul(banks[g][:, 0:GC], V_T, y, start=True, stop=True).then_inc(z_mm[g], 1)

            pe.wait_ge(bn_ok, NT)
            pe.wait_ge(v1_ok, NT)
            for b in range(B):
                done = b * (WARM + L)
                with pe.Fori(1, WARM) as w:
                    for g in range(G):
                        pe.wait_ge(y_ok[g], w + done)
                        v_y(g, warm_y[:, g * GC:(g + 1) * GC])
                pe.wait_ge(start_ok, 2 * b + 2)
                for g in range(G):
                    v_y(g, start_y[:, g * GC:(g + 1) * GC])
                with pe.Fori(1, L) as s:
                    for g in range(G):
                        pe.wait_ge(y_ok[g], s + done + WARM)
                        v_y(g, group_of(wx_buf[b % 2], g, s - 1))

            pe.wait_ge(checked, B + 1)
            pe.transpose(banks[2][0:1, 0:C], agree_all[:, :], ident[:, :]).then_inc(flag_mm, 1)

            pe.wait_ge(flag_ok, 1)
            ok = pe.alloc_register("pe_ok")
            pe.reg_load(ok, agree_i[0:1, 0:1])
            with pe.If_eq(ok, 0):
                pe.wait_ge(seq_zero, 1)
                pe.matmul(banks[3][:, 0:B], V_T, seq_y_buf, start=True, stop=True).then_inc(seq_z, 1)
                with pe.Fori(1, T) as k:
                    pe.wait_ge(seq_y, k)
                    pe.matmul(banks[3][:, 0:B], V_T, seq_y_buf, start=True, stop=True).then_inc(seq_z, 1)
            with pe.Else():
                pe.nop()

        @block.vector
        def _(dve):
            dve.wait_ge(pool_prep, 3)
            dve.wait_ge(weights_in, 16 * PREP_DMAS)
            dve.tensor_scalar(center[:, :], ident[:, :], -1.0 / C, None, ALU.add).then_inc(dve_prep, 1)
            dve.tensor_scalar(kg0[:, :], g0, KAPPA, None, ALU.mult).then_inc(dve_prep, 1)
            dve.wait_ge(dve_prep, 2)
            dve.tensor_scalar(sq1[:, 0:C], center[:, :], kg0[:, 0:1], None, ALU.mult).then_inc(dve_prep, 1)
            dve.tensor_copy(center_r[:, :], center[:, :]).then_inc(dve_prep, 1)
            dve.wait_ge(pe_prep, 1)
            dve.tensor_copy(sq0, p_xc[:, :]).then_inc(dve_prep, 1)
            dve.tensor_copy(value_T[:, :], p_m1[:, :]).then_inc(dve_prep, 1)
            dve.tensor_copy(small_T[:, :], p_var[:, :]).then_inc(dve_prep, 1)
            dve.wait_ge(pe_prep, 2)
            dve.tensor_copy(sq2, p_ha[:, :]).then_inc(dve_prep, 1)
            dve.tensor_copy(sqe[:, 0:C], p_hb[:, 0:C]).then_inc(dve_prep, 1)
            dve.tensor_copy(pb0[:, :], p_t[:, 2 * C:2 * C + 1]).then_inc(dve_prep, 1)
            dve.tensor_copy(m1_hi[:, :], p_t[:, 0:C]).then_inc(dve_prep, 1)
            dve.tensor_copy(wf_hi[:, :], p_t[:, C:2 * C]).then_inc(dve_prep, 1)
            dve.wait_ge(dve_prep, 12)
            dve.tensor_tensor(m1_lo[:, :], p_t[:, 0:C], m1_hi[:, :].bitcast(f32), ALU.subtract).then_inc(dve_prep, 1)
            dve.tensor_tensor(wf_lo[:, :], p_t[:, C:2 * C], wf_hi[:, :].bitcast(f32), ALU.subtract).then_inc(dve_prep, 1)
            dve.wait_ge(pe_prep, 3)
            dve.tensor_copy(hid_bias[:, :], p_kv[:, 0:HB + 1]).then_inc(dve_prep, 1)
            dve.tensor_scalar(rs0, sq2, g2, None, ALU.mult).then_inc(dve_prep, 1)
            dve.tensor_scalar(rs1[:, 0:C], sqe[:, 0:C], g2, None, ALU.mult).then_inc(dve_prep, 1)
            dve.wait_ge(dve_prep, 17)
            dve.tensor_copy(key_hi[:, :], rs0).then_inc(dve_prep, 1)
            dve.tensor_copy(rec_hi[:, :], rs1[:, 0:C]).then_inc(dve_prep, 1)
            dve.wait_ge(dve_prep, 19)
            dve.tensor_tensor(key_lo[:, :], rs0, key_hi[:, :].bitcast(f32), ALU.subtract)
            dve.tensor_tensor(rec_lo[:, :], rs1[:, 0:C], rec_hi[:, :].bitcast(f32), ALU.subtract).then_inc(dve_prep, 1)

            def step(base, m):
                n0, n1, n2, n3, nx = m, m - 1, m - 2, m - 3, m + 1
                if live(base, n1):
                    wait(dve, att_mm, base + n1 + 1)
                    wait(dve, t0p_ok, base + n1 + 1)
                    wait(dve, t2_ok, base + n1 - 1)
                    dve.scalar_tensor_tensor(out=t1[n1 % 2], in0=p_t[:, :], scalar=b0, in1=t0p,
                                             op0=ALU.add, op1=ALU.add).then_inc(t1_ok, 1)
                    wait(dve, t1_ok, base + n1 + 1)
                    wait(dve, t1c_mm, base + n1)
                    dve.tensor_copy(t1_hi[:, :], t1[n1 % 2]).then_inc(t1_hi_ok, 1)
                    wait(dve, t1_hi_ok, base + n1 + 1)
                    dve.tensor_tensor(t1_lo[:, :], t1[n1 % 2], t1_hi[:, :].bitcast(f32), ALU.subtract)\
                       .then_inc(t1_lo_ok, 1)
                if live(base, n2):
                    for j in (1, 3):
                        wait(dve, relu_ok, 4 * (base + n2) + j + 1)
                        wait(dve, kva_mm if j == 1 else kv_mm, base + n2)
                        dve.tensor_tensor(hid[j], relu[j], relu[j], ALU.mult).then_inc(k_dve, 1)
                if live(base, nx):
                    wait(dve, x_loaded[nx % 4], ring(base, nx, 4))
                    wait(dve, m1_mm, base + nx)
                    dve.tensor_copy(x_hi[:, :], x_in[nx % 4]).then_inc(x_hi_ok, 1)
                if live(base, n0):
                    wait(dve, rs0_ok, base + n0 + 1)
                    wait(dve, m1_mm, base + n0 + 1)
                    wait(dve, u1_ok, base + n0)
                    dve.tensor_tensor(t0c, p_m1[:, :], rs0, ALU.mult).then_inc(t0c_ok, 1)
                    wait(dve, t1_ok, base + n0)
                    dve.scalar_tensor_tensor(out=t0p, in0=p_xc[:, :], scalar=kg0[:, 0:1], in1=rs0,
                                             op0=ALU.mult, op1=ALU.mult).then_inc(t0p_ok, 1)
                if live(base, n3):
                    wait(dve, rse_ok, base + n3 + 1)
                    wait(dve, wx_mm, base + n3 + 1)
                    wait(dve, wx_stored[n3 % 2], ring(base, n3 - 2, 2))
                    wait(dve, bn_ok, base + n3 - 1)
                    dve.tensor_tensor(wx[n3 % 2].rearrange("p (s c) -> p c s", c=CPT),
                                      p_x[:, :].rearrange("p (c s) -> p c s", s=L),
                                      rse.rearrange("p (c s) -> p c s", s=L), ALU.mult).then_inc(wx_ok, 1)
                    wait(dve, wx_ok, base + n3 + 1)
                    dve.bn_stats(bn_parts[:, bass.ds((base + n3) * 6, 6)], wx[n3 % 2]).then_inc(bn_ok, 1)
                if live(base, n1):
                    wait(dve, rs2_ok, base + n1 + 1)
                    wait(dve, t1c_mm, base + n1 + 1)
                    wait(dve, y2_lo_ok, base + n1)
                    dve.tensor_tensor(y2, p_t[:, :], rs2, ALU.mult).then_inc(y2_ok, 1)
                    wait(dve, y2_ok, base + n1 + 1)
                    wait(dve, hid_mm, 4 * (base + n1))
                    dve.tensor_copy(y2_hi[:, :], y2).then_inc(y2_hi_ok, 1)
                    wait(dve, y2_hi_ok, base + n1 + 1)
                    dve.tensor_tensor(y2_lo[:, :], y2, y2_hi[:, :].bitcast(f32), ALU.subtract).then_inc(y2_lo_ok, 1)
                if live(base, n0):
                    wait(dve, rs1_ok, base + n0 + 1)
                    wait(dve, t0c_ok, base + n0 + 1)
                    wait(dve, sg_ok, base + n0)
                    dve.scalar_tensor_tensor(out=u1, in0=t0c, scalar=pb0[:, 0:1], in1=rs1,
                                             op0=ALU.add, op1=ALU.mult).then_inc(u1_ok, 1)
                    wait(dve, u1_ok, base + n0 + 1)
                    wait(dve, gate_ok, base + n0)
                    dve.tensor_scalar(y1, u1, g1, b1, ALU.mult, ALU.add).then_inc(y1_ok, 1)
                if live(base, n2):
                    wait(dve, kv_mm, base + n2 + 1)
                    wait(dve, recep_ok, base + n2 + 1)
                    wait(dve, t2_ok, base + n2)
                    dve.tensor_tensor(rkv, p_kv[:, :], recep[n2 % 2], ALU.mult).then_inc(rkv_ok, 1)
                if live(base, n0):
                    wait(dve, sg_ok, base + n0 + 1)
                    wait(dve, y1_ok, base + n0 + 1)
                    wait(dve, att_mm, base + n0)
                    dve.tensor_tensor(gate, y1, sg, ALU.mult).then_inc(gate_ok, 1)
                if live(base, n2):
                    wait(dve, t2_ok, base + n2 + 1)
                    wait(dve, xp_stored[n2 % 2], ring(base, n2 - 2, 2))
                    wait(dve, xp_lo_ok, base + n2 - 1)
                    dve.scalar_tensor_tensor(out=xp[n2 % 2], in0=t2, scalar=2.0, in1=x_in[n2 % 4],
                                             op0=ALU.mult, op1=ALU.add).then_inc(xp_ok, 1)
                    wait(dve, xp_ok, base + n2 + 1)
                    wait(dve, wx_mm, base + n2)
                    dve.tensor_copy(xp_hi[:, :], xp[n2 % 2]).then_inc(xp_hi_ok, 1)

            phase1(dve, step)

            dve.wait_ge(bn_ok, NT)
            dve.bn_aggr(bn_mv[:, :], bn_parts[:, :]).then_inc(bn_dve, 1)
            dve.wait_ge(bn_dve, 1)
            dve.tensor_scalar(bn_small[:, 0:1], bn_mv[:, 1:2], LN_EPS, None, ALU.add).then_inc(bn_dve, 1)
            dve.wait_ge(bn_pool, 1)
            dve.tensor_tensor(bn_scale[:, :], gamma, bn_small[:, 1:2], ALU.mult).then_inc(bn_dve, 1)
            dve.wait_ge(bn_dve, 3)
            dve.tensor_tensor(bn_small[:, 2:3], bn_mv[:, 0:1], bn_scale[:, :], ALU.mult).then_inc(bn_dve, 1)
            dve.wait_ge(bn_dve, 4)
            dve.tensor_tensor(bn_bias[:, :], beta, bn_small[:, 2:3], ALU.subtract).then_inc(bn_ready, 1)

            for b in range(B):
                buf = wx_buf[b % 2]
                done = b * (WARM - 1 + L)
                y_done = b * (WARM + L)

                def argument(g, s, count):
                    dve.wait_ge(z_mm[g], count)
                    dve.scalar_tensor_tensor(out=cols(pre[:, g * GC:(g + 1) * GC]), in0=group_of(buf, g, s),
                                             scalar=bn_scale[:, 0:1], in1=cols(banks[g][:, 0:GC]),
                                             op0=ALU.mult, op1=ALU.add).then_inc(pre_ok[g], 1)

                dve.wait_ge(bn_ready, 1)
                dve.wait_ge(wx_back[b % 2], 16 * (b // 2 + 1))
                with dve.Fori(1, WARM) as w:
                    for g in range(G):
                        argument(g, w + (L - WARM), w + done)
                for g in range(G):
                    dve.wait_ge(y_ok[g], y_done + WARM)
                dve.tensor_copy(start_y[:, 1:NC], warm_y[:, 0:NC - 1]).then_inc(start_ok, 1)
                dve.memset(start_y[:, 0:1], 0.0).then_inc(start_ok, 1)
                for g in range(G):
                    argument(g, 0, done + WARM)
                with dve.Fori(1, L) as s:
                    for g in range(G):
                        argument(g, s, s + done + WARM)
                for g in range(G):
                    dve.wait_ge(y_ok[g], y_done + WARM + L)
                dve.tensor_tensor(cols(diff[:, :]), by_step(buf)[:, :, L - 1, :], cols(warm_y[:, :]), ALU.subtract)\
                   .then_inc(checked_part, 1)
                dve.wait_ge(checked_part, 4 * b + 1)
                dve.tensor_tensor(diff[:, :], diff[:, :], diff[:, :], ALU.mult).then_inc(checked_part, 1)
                dve.wait_ge(checked_part, 4 * b + 2)
                dve.tensor_scalar(diff[:, :], diff[:, :], TOL * TOL, None, ALU.is_le).then_inc(checked_part, 1)
                dve.wait_ge(checked_part, 4 * b + 3)
                dve.tensor_reduce(agree[:, b:b + 1], diff[:, :], AX.X, ALU.min).then_inc(checked, 1)
                dve.wait_ge(checked, b + 1)
                dve.nop().then_inc(checked_part, 1)

            dve.tensor_reduce(agree_all[:, :], agree[:, :], AX.X, ALU.min).then_inc(checked, 1)
            dve.wait_ge(flag_mm, 1)
            dve.tensor_reduce(agree_f[:, :], banks[2][0:1, 0:C], AX.X, ALU.min).then_inc(flag_part, 1)
            dve.wait_ge(flag_part, 1)
            dve.tensor_copy(agree_i[:, :], agree_f[:, :]).then_inc(flag_ok, 1)

            dve.wait_ge(flag_ok, 1)
            ok = dve.alloc_register("dve_ok")
            dve.reg_load(ok, agree_i[0:1, 0:1])
            with dve.If_eq(ok, 0):
                dve.memset(seq_y_buf, 0.0).then_inc(seq_zero, 1)
                with dve.Fori(0, TPB) as t:
                    with dve.Fori(0, CPT) as c:
                        with dve.Fori(0, L) as s:
                            k = t * N + c * L + s
                            dve.wait_ge(seq_in, (t + 1) * 32)
                            dve.wait_ge(seq_z, k + 1)
                            dve.scalar_tensor_tensor(out=seq_pre_buf, in0=seq_wx[:, :, bass.ds(s * CPT + c, 1)]
                                                     .rearrange("p b o -> p (b o)"),
                                                     scalar=bn_scale[:, 0:1], in1=banks[3][:, 0:B],
                                                     op0=ALU.mult, op1=ALU.add).then_inc(seq_pre, 1)
                            dve.wait_ge(seq_y, k + 1)
                            at = seq_xp[:, :, bass.ds(c * L + s, 1)].rearrange("p b o -> p (b o)")
                            dve.tensor_tensor(at, at, seq_y_buf, ALU.add).then_inc(seq_add, 1)
            with dve.Else():
                dve.nop()

        @block.scalar
        def _(act):
            act.wait_ge(dve_prep, 20)

            def variance(v, eps, ready, buf, free, done, base, n):
                wait(act, ready, base + n + 1)
                wait(act, free, base + n)
                act.activation(buf, v, ACT.Identity, bias=eps).then_inc(done, 1)

            def step(base, m):
                n0, n1, n2, n3 = m, m - 1, m - 2, m - 3
                if live(base, n0):
                    wait(act, xc_mm, base + n0 + 1)
                    wait(act, v0_mm, base + n0)
                    act.activation(sq0, p_xc[:, :], ACT.Square).then_inc(sq0_ok, 1)
                if live(base, n3):
                    wait(act, xpc_mm, base + n3 + 1)
                    wait(act, ve_mm, base + n3)
                    act.activation(sqe, p_x[:, :], ACT.Square).then_inc(sqe_ok, 1)
                if live(base, n2):
                    wait(act, relu_ok, 4 * (base + n2) + 1)
                    wait(act, kva_mm, base + n2)
                    act.activation(hid[0], relu[0], ACT.Square).then_inc(k_act, 1)
                if live(base, n0):
                    variance(p_var[:, :], EPS0, v0_mm, v0, rs0_ok, v0_ok, base, n0)
                if live(base, n1):
                    wait(act, t1c_mm, base + n1 + 1)
                    wait(act, v2_mm, base + n1)
                    act.activation(sq2, p_t[:, :], ACT.Square).then_inc(sq2_ok, 1)
                if live(base, n3):
                    variance(p_var[:, :], LN_EPS, ve_mm, ve, rse_ok, ve_ok, base, n3)
                if live(base, n1):
                    variance(p_var[:, :], LN_EPS, v2_mm, v2, rs2_ok, v2_ok, base, n1)
                if live(base, n0):
                    wait(act, t0c_ok, base + n0 + 1)
                    wait(act, v1_mm, base + n0)
                    act.activation(sq1, t0c, ACT.Square, bias=pb0[:, 0:1]).then_inc(sq1_ok, 1)
                if live(base, n2):
                    wait(act, relu_ok, 4 * (base + n2) + 3)
                    wait(act, kv_mm, base + n2)
                    act.activation(hid[2], relu[2], ACT.Square).then_inc(k_act, 1)
                if live(base, n0):
                    variance(p_var[:, :], LN_EPS, v1_mm, v1, rs1_ok, v1_ok, base, n0)
                if live(base, n1):
                    wait(act, rec_mm, base + n1 + 1)
                    wait(act, rkv_ok, base + n1 - 1)
                    act.activation(recep[n1 % 2], p_ha[:, :], ACT.Sigmoid, bias=hid_bias[:, HB:HB + 1])\
                       .then_inc(recep_ok, 1)
                if live(base, n0):
                    wait(act, u1_ok, base + n0 + 1)
                    wait(act, gate_ok, base + n0)
                    act.activation(sg, u1, ACT.Sigmoid, bias=b1, scale=g1).then_inc(sg_ok, 1)
                if live(base, n1):
                    for j in range(HB):
                        wait(act, hid_mm, 4 * (base + n1) + j + 1)
                        wait(act, k_dve if j % 2 else k_act, 2 * (base + n1) - 1 + j // 2)
                        act.activation(relu[j], (p_hb, p_ha)[j % 2][:, :], ACT.Relu, bias=hid_bias[:, j:j + 1])\
                           .then_inc(relu_ok, 1)

            phase1(act, step)

            act.wait_ge(bn_ready, 1)
            for b in range(B):
                buf = wx_buf[b % 2]
                done = b * (WARM - 1 + L)

                def state(g, dst, count):
                    act.wait_ge(pre_ok[g], count)
                    act.activation(dst, cols(pre[:, g * GC:(g + 1) * GC]), ACT.Sigmoid, bias=bn_bias[:, 0:1])\
                       .then_inc(y_ok[g], 1)

                act.wait_ge(wx_back[b % 2], 16 * (b // 2 + 1))
                if b:
                    act.wait_ge(checked, b)
                for g in range(G):
                    act.activation(cols(warm_y[:, g * GC:(g + 1) * GC]), group_of(buf, g, L - WARM), ACT.Sigmoid,
                                   bias=bn_bias[:, 0:1], scale=bn_scale[:, 0:1]).then_inc(y_ok[g], 1)
                with act.Fori(1, WARM) as w:
                    for g in range(G):
                        state(g, cols(warm_y[:, g * GC:(g + 1) * GC]), w + done)
                for g in range(G):
                    state(g, group_of(buf, g, 0), done + WARM)
                with act.Fori(1, L) as s:
                    for g in range(G):
                        state(g, group_of(buf, g, s), s + done + WARM)

            act.wait_ge(flag_ok, 1)
            ok = act.alloc_register("act_ok")
            act.reg_load(ok, agree_i[0:1, 0:1])
            with act.If_eq(ok, 0):
                with act.Fori(0, T) as k:
                    act.wait_ge(seq_pre, k + 1)
                    act.activation(seq_y_buf, seq_pre_buf, ACT.Sigmoid, bias=bn_bias[:, 0:1]).then_inc(seq_y, 1)
            with act.Else():
                act.nop()

        @block.gpsimd
        def _(pool):
            pool.memset(ident[:, :], 0.0).then_inc(pool_prep, 1)
            pool.memset(mean_w[:, :], 1.0 / C)
            pool.memset(neg_half[:, :], -0.5).then_inc(pool_prep, 1)
            pool.wait_ge(pool_prep, 2)
            pool.affine_select(out=ident[:, :], in_=ident[:, :], compare_op=ALU.not_equal, fill=1.0,
                               base=0, pattern=[[-1, C]], channel_multiplier=1).then_inc(pool_prep, 1)
            pool.wait_ge(dve_prep, 20)

            def inv_root(v, ready, rs, free, done, base, n):
                wait(pool, ready, base + n + 1)
                for s in free:
                    wait(pool, s, base + n)
                pool.tensor_tensor(rs, v, neg_half[:, :], ALU.pow).then_inc(done, 1)

            def step(base, m):
                n0, n1, n2, n3, nx = m, m - 1, m - 2, m - 3, m + 1
                if live(base, n0):
                    inv_root(v0, v0_ok, rs0, (t0p_ok,), rs0_ok, base, n0)
                if live(base, n3):
                    inv_root(ve, ve_ok, rse, (wx_ok,), rse_ok, base, n3)
                if live(base, n1):
                    inv_root(v2, v2_ok, rs2, (y2_ok,), rs2_ok, base, n1)
                if live(base, nx):
                    wait(pool, x_hi_ok, base + nx + 1)
                    wait(pool, m1_mm, base + nx)
                    pool.tensor_tensor(x_lo[:, :], x_in[nx % 4], x_hi[:, :].bitcast(f32), ALU.subtract)\
                        .then_inc(x_lo_ok, 1)
                if live(base, n0):
                    inv_root(v1, v1_ok, rs1, (u1_ok,), rs1_ok, base, n0)
                if live(base, n2):
                    wait(pool, rkv_ok, base + n2 + 1)
                    wait(pool, xp_ok, base + n2)
                    pool.tensor_tensor(t2, rkv, t1[n2 % 2], ALU.add).then_inc(t2_ok, 1)
                    wait(pool, xp_hi_ok, base + n2 + 1)
                    wait(pool, wx_mm, base + n2)
                    pool.tensor_tensor(xp_lo[:, :], xp[n2 % 2], xp_hi[:, :].bitcast(f32), ALU.subtract)\
                        .then_inc(xp_lo_ok, 1)

            phase1(pool, step)

            pool.wait_ge(bn_dve, 2)
            pool.tensor_tensor(bn_small[:, 1:2], bn_small[:, 0:1], neg_half[:, 0:1], ALU.pow).then_inc(bn_pool, 1)

            for b in range(B):
                for g in range(G):
                    pool.wait_ge(y_ok[g], (b + 1) * (WARM + L))
                for t in range(TPB):
                    k = (b * TPB + t) // 4
                    if t % 4 == 0:
                        pool.wait_ge(stage_in[k % 3], 16 * (k // 3 + 1))
                    at = stage[:, ((k % 3) * 4 + t % 4) * N:((k % 3) * 4 + t % 4 + 1) * N]\
                        .rearrange("p (c s) -> p c s", s=L)
                    pool.tensor_tensor(at, at, wx_buf[b % 2][:, t * N:(t + 1) * N]
                                       .rearrange("p (s c) -> p c s", c=CPT), ALU.add).then_inc(added, 1)


_INS = ['x', 'L0_conv_ln0_g', 'L0_conv_ln0_b', 'L0_conv_ln1_g', 'L0_conv_ln1_b', 'L0_conv_ln2_g',
        'L0_conv_ln2_b', 'L0_conv_W_out', 'L0_conv_W_whiten', 'L0_conv_W_key', 'L0_conv_W_recep',
        'L0_conv_W_value', 'L0_ffn_W', 'L0_ffn_V', 'L0_ffn_gamma', 'L0_ffn_beta']


def kernel(**inputs):
    import numpy as np
    import concourse.bacc as bacc
    from concourse.bass_utils import run_bass_kernel_spmd

    nc = bacc.Bacc("TRN2", target_bir_lowering=False, num_devices=1)
    arrays, args = {}, []
    for name in _INS:
        a = np.ascontiguousarray(inputs[name])
        arrays[f"in_{name}"] = a
        args.append(nc.dram_tensor(f"in_{name}", a.shape, mybir.dt.from_np(a.dtype), kind="ExternalInput").ap())
    out = nc.dram_tensor("out", arrays["in_x"].shape, mybir.dt.float32, kind="ExternalOutput")
    metaformer_kernel(nc, *args, out.ap())
    r = run_bass_kernel_spmd(nc, [arrays], core_ids=[0])
    return r.results[0]["out"]
```

```python
import concourse.bass as bass
from concourse import mybir
from contextlib import ExitStack


def metaformer_kernel(nc, x, ln0_g, ln0_b, ln1_g, ln1_b, ln2_g, ln2_b,
                      W_out, W_whiten, W_key, W_recep, W_value,
                      W_ffn, V_ffn, bn_gamma, bn_beta, out):
    f32, f32r, i32 = mybir.dt.float32, mybir.dt.float32r, mybir.dt.int32
    ALU, ACT, AX = mybir.AluOpType, mybir.ActivationFunctionType, mybir.AxisListType

    B, C, H, Wd = x.shape
    T = H * Wd
    N = 512
    NT = B * T // N
    TPB = T // N
    HB = W_key.shape[0] // C
    L = 32
    CPT = N // L
    NC = T // L
    BLK = N // C
    WARM = 14
    TOL = 2.0 ** -21
    G = 2
    GC = NC // G
    GT = TPB // G
    LN_EPS = 1e-5
    KAPPA = (1.0 + LN_EPS) ** -0.5
    EPS0 = LN_EPS * 1e-6 / (1.0 + LN_EPS)

    x_d = x.rearrange("b c h w -> b c (h w)")
    out_d = out.rearrange("b c h w -> b c (h w)")
    xp_d = nc.dram_tensor("x_prime", (C, NT * N), f32, kind="Internal").ap()
    wx_d = nc.dram_tensor("w_x", (C, NT * N), f32, kind="Internal").ap()

    ctx = ExitStack()
    with ctx:
        def sb(name, cols, dt=f32, rows=C):
            return ctx.enter_context(nc.sbuf_tensor(name, [rows, cols], dt))

        def sem(name):
            return ctx.enter_context(nc.semaphore(name))

        def sems(name, n):
            return [sem(f"{name}{i}") for i in range(n)]

        ident = sb("ident", C)
        center = sb("center", C)
        neg_half = sb("neg_half", BLK)
        vecs = sb("vecs", 8)
        g1, b1, g2, b2, gamma, beta = (vecs[:, k:k + 1] for k in range(2, 8))
        ln0_rows = sb("ln0_rows", 2 * N)
        g0_row, b0_row = ln0_rows[:, 0:N], ln0_rows[:, N:2 * N]
        hid_bias = sb("hid_bias", HB + 1)
        key_hi, key_lo = sb("key_hi", HB * C, f32r), sb("key_lo", HB * C, f32r)
        rec_hi, rec_lo = sb("rec_hi", C, f32r), sb("rec_lo", C, f32r)
        wf_T = sb("wf_T", C)
        value_T = sb("value_T", HB * C)
        small_T = sb("small_T", 4 * C)
        out_T, rec_T, ffn_T, V_T = (small_T[:, k * C:(k + 1) * C] for k in range(4))

        y2_hi, y2_lo = sb("y2_hi", N, f32r), sb("y2_lo", N, f32r)

        wx_even = sb("wx_even", T)
        arena = sb("arena", 44 * N)
        wx_buf = [wx_even[:, :], arena[:, 0:T]]
        arena_at = [0]

        def tile(n=1):
            at = arena_at[0]
            arena_at[0] += n
            return [arena[:, (at + k) * N:(at + k + 1) * N] for k in range(n)]

        x_in = tile(8)
        (xn,), (xg,), (t0,), (u,), (t0_c,) = (tile() for _ in range(5))
        (sg,), (y1,), (gate,), (y2,) = (tile() for _ in range(4))
        t1 = tile(4)
        relu = tile(HB)
        hid = tile(HB)
        recep = tile(2)
        (rkv,), (t2,) = tile(), tile()
        xp = tile(2)
        (un,), (un_c,) = tile(), tile()
        wx = tile(2)
        assert arena_at[0] <= 44

        stage = arena[:, T:T + 3 * 4 * N]
        LNS = ("0", "1", "2", "e")
        st = {k: sb(f"st{k}", BLK * 6) for k in LNS}
        mv = {k: sb(f"mv{k}", BLK * 2) for k in LNS}
        veps = {k: sb(f"veps{k}", BLK) for k in LNS}
        rs = {k: sb(f"rs{k}", BLK) for k in LNS}
        shift0 = sb("shift0", BLK)

        bn_parts = sb("bn_parts", NT * 6)
        bn_mv = sb("bn_mv", 2)
        bn_small = sb("bn_small", 3)
        bn_scale = sb("bn_scale", 1)
        bn_bias = sb("bn_bias", 1)
        warm_y = sb("warm_y", NC)
        start_y = sb("start_y", NC)
        pre = sb("pre", NC)
        diff = pre
        agree = sb("agree", B)
        agree_all = sb("agree_all", 1)
        agree_f = sb("agree_f", 1, rows=1)
        agree_i = sb("agree_i", 1, i32, rows=1)

        banks = [ctx.enter_context(nc.psum_tensor(f"bank{k}", [C, N], f32)) for k in range(8)]
        p_x, p_t1, p_xp, p_u, p_ha, p_hb, p_kv, p_wx = banks

        weights_in, pool_prep, dve_prep, pe_prep = (sem(n) for n in ("weights_in", "pool_prep", "dve_prep", "pe_prep"))
        x_loaded = sems("x_loaded", 8)
        xp_stored = sems("xp_stored", 2)
        wx_stored = sems("wx_stored", 2)
        var_ok = {k: sem(f"var{k}_ok") for k in LNS}
        mv_part = {k: sem(f"mv{k}_part") for k in LNS}
        aggr_turn = sem("aggr_turn")
        shift0_ok, u_ok, y2_ok, un_ok, gate_ok, y2_lo_ok, rkv_ok, t1_ok, xp_ok, bn_ok = (
            sem(n) for n in ("shift0_ok", "u_ok", "y2_ok", "un_ok", "gate_ok", "y2_lo_ok", "rkv_ok", "t1_ok", "xp_ok", "bn_ok"))
        rs_ok = {k: sem(f"rs{k}_ok") for k in LNS}
        xg_ok, t0_ok, t2_ok = (sem(n) for n in ("xg_ok", "t0_ok", "t2_ok"))
        hid_ok, t0_c_ok, sg_ok, y1_ok, xn_ok, y2_hi_ok, un_c_ok, recep_ok, relu_ok, wx_ok = (
            sem(n) for n in ("hid_ok", "t0_c_ok", "sg_ok", "y1_ok", "xn_ok", "y2_hi_ok", "un_c_ok", "recep_ok", "relu_ok", "wx_ok"))
        x_tr, t1_tr, xp_tr, t0_tr, u_tr, y2_tr, un_tr = (
            sem(n) for n in ("x_tr", "t1_tr", "xp_tr", "t0_tr", "u_tr", "y2_tr", "un_tr"))
        att_mm, rec_mm, hid_mm, kva_mm, kv_mm, wx_mm = (
            sem(n) for n in ("att_mm", "rec_mm", "hid_mm", "kva_mm", "kv_mm", "wx_mm"))
        bn_dve, bn_pool, bn_ready = sem("bn_dve"), sem("bn_pool"), sem("bn_ready")
        wx_back = sems("wx_back", 2)
        stage_in = sems("stage_in", 3)
        stage_out = sems("stage_out", 3)
        z_mm, pre_ok, y_ok = sems("z_mm", G), sems("pre_ok", G), sems("y_ok", G)
        start_ok, added, checked, checked_part, flag_mm, flag_part, flag_ok = (
            sem(n) for n in ("start_ok", "added", "checked", "checked_part", "flag_mm", "flag_part", "flag_ok"))
        seq_in, seq_out, seq_free, seq_z, seq_pre, seq_y, seq_add, seq_zero = (
            sem(n) for n in ("seq_in", "seq_out", "seq_free", "seq_z", "seq_pre", "seq_y", "seq_add", "seq_zero"))

        PREP_DMAS = 8 + 2 * BLK + 7

        LAG = 4
        LOOP = (0, NT - 8)
        PER_LOOP = range(7, 15)

        def phase1(eng, step):
            for i in range(PER_LOOP[0]):
                step(0, i)
            with eng.Fori(LOOP[0], LOOP[1] - 7, 8) as base:
                for m in PER_LOOP:
                    step(base, m)
            for i in range(LOOP[1] + PER_LOOP[0], NT + LAG):
                step(0, i)

        def live(base, n):
            return not isinstance(base, int) or 0 <= base + n < NT

        def wait(eng, s, count):
            if not isinstance(count, int) or count > 0:
                eng.wait_ge(s, count)

        def ring(base, m, size, each=16):
            return base * (each // size) + each * (m // size + 1)

        seq_wx = wx_even[:, 0:B * N].rearrange("c (b n) -> c b n", b=B)
        seq_xp = wx_even[:, B * N:2 * B * N].rearrange("c (b n) -> c b n", b=B)
        seq_y_buf = start_y[:, 0:B]
        seq_pre_buf = pre[:, 0:B]

        def blocks(ap):
            return ap.rearrange("p (j c) -> p j c", c=C)

        def by_block(buf):
            return buf[:, :].rearrange("p (j k) -> p j k", j=BLK)

        def per_token(ap):
            return ap.unsqueeze(2).to_broadcast([C, BLK, C])

        def by_step(buf):
            return buf.rearrange("p (t s c) -> p t s c", s=L, c=CPT)

        def group_of(buf, g, s):
            return by_step(buf)[:, g * GT:(g + 1) * GT, bass.ds(s, 1), :].rearrange("p t s c -> p (t s) c")

        def cols(ap):
            return ap.rearrange("p (t c) -> p t c", c=CPT)

        block = ctx.enter_context(nc.Block())

        @block.sync
        def _(sp):
            for k, v in enumerate((ln0_g, ln0_b, ln1_g, ln1_b, ln2_g, ln2_b, bn_gamma, bn_beta)):
                sp.dma_start(vecs[:, k:k + 1], v.rearrange("(c o) -> c o", o=1)).then_inc(weights_in, 16)
            for k, v in enumerate((ln0_g, ln0_b)):
                for j in range(BLK):
                    at = k * N + j * C
                    sp.dma_start(ln0_rows[:, at:at + C], v.partition_broadcast(C)).then_inc(weights_in, 16)
            sp.dma_start(hid[0][:, :].rearrange("p (j c) -> p j c", c=C),
                         W_key.rearrange("(j p) c -> p j c", p=C)).then_inc(weights_in, 16)
            sp.dma_start(hid[1][:, :], W_value).then_inc(weights_in, 16)
            for k, w in enumerate((W_out, W_recep, W_ffn, V_ffn)):
                sp.dma_start(hid[2][:, k * C:(k + 1) * C], w).then_inc(weights_in, 16)
            sp.dma_start(hid[3][:, 0:C], W_whiten).then_inc(weights_in, 16)

            def load_and_store(b, base, m):
                if live(base, m - 8):
                    wait(sp, xp_ok, base + m - 7)
                if live(base, m):
                    col = (base + m - b * TPB) * N
                    sp.dma_start(x_in[m % 8], x_d[b, :, bass.ds(col, N)]).then_inc(x_loaded[m % 8], 16)
                if live(base, m - 8):
                    sp.dma_start(xp_d[:, bass.ds((base + m - 8) * N, N)], xp[m % 2]).then_inc(xp_stored[m % 2], 16)
                if live(base, m - 9):
                    wait(sp, wx_ok, base + m - 8)
                    sp.dma_start(wx_d[:, bass.ds((base + m - 9) * N, N)], wx[(m - 9) % 2])\
                      .then_inc(wx_stored[(m - 9) % 2], 16)

            for m in range(16):
                load_and_store(0, 0, m)
            for b in range(B):
                if b == 2:
                    for s in wx_stored:
                        sp.wait_ge(s, 16 * TPB // 2)
                    sp.dma_start(wx_buf[0], wx_d[:, 0:T]).then_inc(wx_back[0], 16)
                with sp.Fori(max(b * TPB, 16), (b + 1) * TPB - 7, 8) as base:
                    for m in range(8):
                        load_and_store(b, base, m)
            for m in range(NT, NT + 9):
                load_and_store(B - 1, 0, m)

            for s in xp_stored + wx_stored:
                sp.wait_ge(s, 16 * NT // 2)
            sp.wait_ge(bn_ok, NT)
            sp.dma_start(wx_buf[1], wx_d[:, T:2 * T]).then_inc(wx_back[1], 16)
            SW = 4 * N
            NS = NT // 4

            def stage_load(k):
                if k >= 3:
                    sp.wait_ge(stage_out[k % 3], 16 * (k // 3))
                sp.dma_start(stage[:, (k % 3) * SW:(k % 3 + 1) * SW], xp_d[:, k * SW:(k + 1) * SW])\
                  .then_inc(stage_in[k % 3], 16)

            stage_load(0)
            stage_load(1)
            for k in range(NS):
                if k + 2 < NS:
                    stage_load(k + 2)
                sp.wait_ge(added, 4 * (k + 1))
                b, col = k // (TPB // 4), k % (TPB // 4) * SW
                sp.dma_start(out_d[b, :, col:col + SW], stage[:, (k % 3) * SW:(k % 3 + 1) * SW])\
                  .then_inc(stage_out[k % 3], 16)
                if (k + 1) % (TPB // 4) == 0 and b + 2 < B:
                    sp.wait_ge(checked, b + 1)
                    sp.dma_start(wx_buf[b % 2], wx_d[:, (b + 2) * T:(b + 3) * T]).then_inc(wx_back[b % 2], 16)
            for s in range(3):
                sp.wait_ge(stage_out[s], 16 * ((NS - 1 - s) // 3 + 1))

            sp.wait_ge(flag_ok, 1)
            ok = sp.alloc_register("sp_ok")
            sp.reg_load(ok, agree_i[0:1, 0:1])
            with sp.If_eq(ok, 0):
                with sp.Fori(0, TPB) as t:
                    for dst, src in ((seq_wx, wx_d), (seq_xp, xp_d)):
                        sp.dma_start(dst, src.rearrange("c (b n) -> c b n", b=B)[:, :, bass.ds(t * N, N)])\
                          .then_inc(seq_in, 16)
                    sp.wait_ge(seq_add, (t + 1) * N)
                    sp.dma_start(out_d.rearrange("b c n -> c b n")[:, :, bass.ds(t * N, N)], seq_xp)\
                      .then_inc(seq_out, 16)
                    sp.wait_ge(seq_out, (t + 1) * 16)
                    sp.sem_inc(seq_free, 1)
            with sp.Else():
                sp.nop()

        @block.tensor
        def _(pe):
            pe.wait_ge(weights_in, 16 * PREP_DMAS)
            pe.wait_ge(pool_prep, 3)
            for j in range(HB):
                pe.transpose(p_x[:, j * C:(j + 1) * C], hid[0][:, j * C:(j + 1) * C], ident[:, :])
                pe.transpose(p_t1[:, j * C:(j + 1) * C], hid[1][:, j * C:(j + 1) * C], ident[:, :])
                mm = pe.transpose(p_xp[:, j * C:(j + 1) * C], hid[2][:, j * C:(j + 1) * C], ident[:, :])
            mm.then_inc(pe_prep, 1)
            pe.wait_ge(dve_prep, 5)
            pe.matmul(p_u[:, 0:C], center[:, :], ffn_T, start=True, stop=True)
            pe.matmul(p_ha[:, :], hid[3][:, 0:C], sg, start=True, stop=True)
            pe.matmul(p_hb[:, 0:C], hid[3][:, 0:C], rec_T, start=True, stop=True).then_inc(pe_prep, 1)
            pe.wait_ge(dve_prep, 10)
            for j in range(HB):
                pe.matmul(p_kv[:, j:j + 1], y1[:, j * C:(j + 1) * C], b2, start=True, stop=True)
            pe.matmul(p_kv[:, HB:HB + 1], gate[:, 0:C], b2, start=True, stop=True)
            pe.matmul(p_x[:, :], center[:, :], y2, start=True, stop=True)
            pe.matmul(p_t1[:, 0:C], center[:, :], u[:, 0:C], start=True, stop=True).then_inc(pe_prep, 1)
            pe.wait_ge(dve_prep, 15)

            def turn(bank, tile):
                for j in range(BLK):
                    mm = pe.transpose(bank[:, j * C:(j + 1) * C], tile[:, j * C:(j + 1) * C], ident[:, :])
                return mm

            def mm3(bank, hi, lo, m_hi, m_lo):
                pe.matmul(bank, lo, m_hi, start=True, stop=False)
                pe.matmul(bank, hi, m_lo, start=False, stop=False)
                return pe.matmul(bank, hi, m_hi, start=False, stop=True)

            def step(base, m):
                n0, n1, n2, n3 = (m - k for k in range(4))
                if live(base, n0):
                    wait(pe, x_loaded[n0 % 8], ring(base, n0, 8))
                    wait(pe, xn_ok, base + n0)
                    turn(p_x, x_in[n0 % 8]).then_inc(x_tr, 1)
                if live(base, n1):
                    wait(pe, t0_ok, base + n1 + 1)
                    if live(base, n3 - 1):
                        wait(pe, un_c_ok, base + n3)
                    turn(p_xp, t0).then_inc(t0_tr, 1)
                    wait(pe, u_ok, base + n1 + 1)
                    wait(pe, t1_ok, base + n1)
                    turn(p_u, u).then_inc(u_tr, 1)

                def hidden(blocks_):
                    for j in blocks_:
                        if j == 1:
                            wait(pe, y2_lo_ok, base + n2 + 1)
                        elif j == 2:
                            wait(pe, recep_ok, base + n2 + 1)
                        elif j == 3:
                            wait(pe, relu_ok, 4 * (base + n2) + 1)
                        mm3((p_hb, p_t1, p_ha, p_hb)[j][:, :], key_hi[:, j * C:(j + 1) * C],
                            key_lo[:, j * C:(j + 1) * C], y2_hi[:, :], y2_lo[:, :]).then_inc(hid_mm, 1)

                if live(base, n2):
                    wait(pe, y2_hi_ok, base + n2 + 1)
                    wait(pe, y2_lo_ok, base + n2 + 1)
                    wait(pe, relu_ok, 4 * (base + n2))
                    mm3(p_ha[:, :], rec_hi[:, :], rec_lo[:, :], y2_hi[:, :], y2_lo[:, :]).then_inc(rec_mm, 1)
                    hidden((0, 1))
                if live(base, n3):
                    wait(pe, xp_ok, base + n3 + 1)
                    if live(base, n1):
                        wait(pe, t0_c_ok, base + n1 + 1)
                    else:
                        wait(pe, un_c_ok, base + n3)
                    turn(p_xp, xp[n3 % 2]).then_inc(xp_tr, 1)
                if live(base, n1):
                    wait(pe, gate_ok, base + n1 + 1)
                    pe.matmul(p_u[:, :], out_T, gate, start=True, stop=True).then_inc(att_mm, 1)
                if live(base, n2):
                    hidden((2, 3))
                if live(base, n1):
                    wait(pe, t1_ok, base + n1 + 1)
                    if live(base, n2):
                        wait(pe, relu_ok, 4 * (base + n2) + 2)
                    turn(p_t1, t1[n1 % 4]).then_inc(t1_tr, 1)

                def value(second):
                    for j in range(2 * second, 2 * second + 2):
                        wait(pe, hid_ok, 4 * (base + n2) + j + 1)
                        mm = pe.matmul(p_kv[:, :], value_T[:, j * C:(j + 1) * C], hid[j],
                                       start=(j == 0), stop=(j == HB - 1))
                    mm.then_inc(kv_mm if second else kva_mm, 1)

                if live(base, n2):
                    wait(pe, rkv_ok, base + n2)
                    value(0)
                if live(base, n3):
                    wait(pe, un_ok, base + n3 + 1)
                    turn(p_xp, un).then_inc(un_tr, 1)
                if live(base, n2):
                    value(1)
                if live(base, n1):
                    wait(pe, y2_ok, base + n1 + 1)
                    turn(p_t1, y2).then_inc(y2_tr, 1)
                if live(base, n3):
                    wait(pe, un_c_ok, base + n3 + 1)
                    wait(pe, wx_ok, base + n3)
                    pe.matmul(p_wx[:, :], wf_T[:, :], un_c, start=True, stop=True).then_inc(wx_mm, 1)

            phase1(pe, step)

            def v_y(g, y):
                pe.matmul(banks[g][:, 0:GC], V_T, y, start=True, stop=True).then_inc(z_mm[g], 1)

            pe.wait_ge(bn_ok, NT)
            for b in range(B):
                done = b * (WARM + L)
                with pe.Fori(1, WARM) as w:
                    for g in range(G):
                        pe.wait_ge(y_ok[g], w + done)
                        v_y(g, warm_y[:, g * GC:(g + 1) * GC])
                pe.wait_ge(start_ok, 2 * b + 2)
                for g in range(G):
                    v_y(g, start_y[:, g * GC:(g + 1) * GC])
                with pe.Fori(1, L) as s:
                    for g in range(G):
                        pe.wait_ge(y_ok[g], s + done + WARM)
                        v_y(g, group_of(wx_buf[b % 2], g, s - 1))

            pe.wait_ge(checked, B + 1)
            pe.transpose(banks[2][0:1, 0:C], agree_all[:, :], ident[:, :]).then_inc(flag_mm, 1)

            pe.wait_ge(flag_ok, 1)
            ok = pe.alloc_register("pe_ok")
            pe.reg_load(ok, agree_i[0:1, 0:1])
            with pe.If_eq(ok, 0):
                pe.wait_ge(seq_zero, 1)
                pe.matmul(banks[3][:, 0:B], V_T, seq_y_buf, start=True, stop=True).then_inc(seq_z, 1)
                with pe.Fori(1, T) as k:
                    pe.wait_ge(seq_y, k)
                    pe.matmul(banks[3][:, 0:B], V_T, seq_y_buf, start=True, stop=True).then_inc(seq_z, 1)
            with pe.Else():
                pe.nop()

        @block.vector
        def _(dve):
            dve.wait_ge(pool_prep, 3)
            dve.wait_ge(weights_in, 16 * PREP_DMAS)
            dve.tensor_scalar(center[:, :], ident[:, :], -1.0 / C, None, ALU.add).then_inc(dve_prep, 1)
            dve.tensor_scalar(g0_row, g0_row, KAPPA, None, ALU.mult).then_inc(dve_prep, 1)
            dve.wait_ge(pe_prep, 1)
            dve.tensor_copy(sg, p_x[:, :]).then_inc(dve_prep, 1)
            dve.tensor_copy(value_T[:, :], p_t1[:, :]).then_inc(dve_prep, 1)
            dve.tensor_copy(small_T[:, :], p_xp[:, :]).then_inc(dve_prep, 1)
            dve.wait_ge(pe_prep, 2)
            dve.tensor_copy(wf_T[:, :], p_u[:, 0:C]).then_inc(dve_prep, 1)
            dve.tensor_copy(y1, p_ha[:, :]).then_inc(dve_prep, 1)
            dve.tensor_copy(gate[:, 0:C], p_hb[:, 0:C]).then_inc(dve_prep, 1)
            dve.tensor_scalar(y2, p_ha[:, :], g2, None, ALU.mult).then_inc(dve_prep, 1)
            dve.tensor_scalar(u[:, 0:C], p_hb[:, 0:C], g2, None, ALU.mult).then_inc(dve_prep, 1)
            dve.wait_ge(pe_prep, 3)
            dve.tensor_copy(hid_bias[:, :], p_kv[:, 0:HB + 1]).then_inc(dve_prep, 1)
            dve.tensor_copy(key_hi[:, :], p_x[:, :]).then_inc(dve_prep, 1)
            dve.tensor_copy(rec_hi[:, :], p_t1[:, 0:C]).then_inc(dve_prep, 1)
            dve.wait_ge(dve_prep, 13)
            dve.tensor_tensor(key_lo[:, :], p_x[:, :], key_hi[:, :].bitcast(f32), ALU.subtract).then_inc(dve_prep, 1)
            dve.tensor_tensor(rec_lo[:, :], p_t1[:, 0:C], rec_hi[:, :].bitcast(f32), ALU.subtract).then_inc(dve_prep, 1)

            def sums(k, tile, base, n):
                wait(dve, mv_part[k], 2 * (base + n))
                for j in range(BLK):
                    s_ = dve.bn_stats(st[k][:, 6 * j:6 * j + 6], tile[:, j * C:(j + 1) * C])
                s_.then_inc(mv_part[k], 1)

            def mean_var(k, eps, base, n):
                wait(dve, mv_part[k], 2 * (base + n) + 1)
                dve.sem_inc(aggr_turn, 1)
                for j in range(BLK):
                    s_ = dve.bn_aggr(mv[k][:, 2 * j:2 * j + 2], st[k][:, 6 * j:6 * j + 6])
                s_.then_inc(mv_part[k], 1)
                wait(dve, mv_part[k], 2 * (base + n) + 2)
                wait(dve, rs_ok[k], base + n)
                dve.tensor_scalar(veps[k][:, :], by_block(mv[k])[:, :, 1], eps, None, ALU.add).then_inc(var_ok[k], 1)

            def scale_tokens(dst, k, bank):
                return dve.tensor_tensor(blocks(dst), blocks(bank[:, :]), per_token(rs[k][:, :]), ALU.mult)

            def step(base, m):
                n0, n1, n2, n3, n4 = (m - k for k in range(5))
                if live(base, n2):
                    wait(dve, y2_hi_ok, base + n2 + 1)
                    wait(dve, hid_mm, 4 * (base + n2))
                    dve.tensor_tensor(y2_lo[:, :], p_t1[:, :], y2_hi[:, :].bitcast(f32), ALU.subtract)\
                       .then_inc(y2_lo_ok, 1)
                if live(base, n3):
                    wait(dve, kv_mm, base + n3 + 1)
                    wait(dve, recep_ok, base + n3 + 1)
                    wait(dve, t2_ok, base + n3)
                    dve.tensor_tensor(rkv, p_kv[:, :], recep[n3 % 2], ALU.mult).then_inc(rkv_ok, 1)
                if live(base, n0):
                    wait(dve, x_tr, base + n0 + 1)
                    sums("0", p_x, base, n0)
                    wait(dve, shift0_ok, base + n0)
                    mean_var("0", EPS0, base, n0)
                if live(base, n3):
                    wait(dve, t2_ok, base + n3 + 1)
                    wait(dve, xp_stored[n3 % 2], ring(base, n3 - 2, 2))
                    wait(dve, xp_tr, base + n3 - 1)
                    dve.scalar_tensor_tensor(out=xp[n3 % 2], in0=t2, scalar=2.0, in1=x_in[n3 % 8],
                                             op0=ALU.mult, op1=ALU.add).then_inc(xp_ok, 1)
                if live(base, n1):
                    wait(dve, sg_ok, base + n1 + 1)
                    wait(dve, y1_ok, base + n1 + 1)
                    wait(dve, att_mm, base + n1)
                    dve.tensor_tensor(gate, y1, sg, ALU.mult).then_inc(gate_ok, 1)
                if live(base, n0):
                    wait(dve, rs_ok["0"], base + n0 + 1)
                    wait(dve, xn_ok, base + n0)
                    dve.scalar_tensor_tensor(out=shift0[:, :], in0=by_block(mv["0"])[:, :, 0], scalar=-1.0,
                                             in1=rs["0"][:, :], op0=ALU.mult, op1=ALU.mult).then_inc(shift0_ok, 1)
                if live(base, n3):
                    wait(dve, xp_tr, base + n3 + 1)
                    sums("e", p_xp, base, n3)
                    mean_var("e", LN_EPS, base, n3)
                if live(base, n1):
                    wait(dve, att_mm, base + n1 + 1)
                    wait(dve, t0_c_ok, base + n1 + 1)
                    wait(dve, t2_ok, base + n1 - 3)
                    dve.tensor_tensor(t1[n1 % 4], p_u[:, :], t0_c, ALU.add).then_inc(t1_ok, 1)
                if live(base, n3):
                    wait(dve, rs_ok["e"], base + n3 + 1)
                    wait(dve, un_tr, base + n3)
                    scale_tokens(un, "e", p_xp).then_inc(un_ok, 1)
                if live(base, n1):
                    wait(dve, t1_tr, base + n1 + 1)
                    sums("2", p_t1, base, n1)
                if live(base, n4):
                    wait(dve, wx_ok, base + n4 + 1)
                    dve.bn_stats(bn_parts[:, bass.ds((base + n4) * 6, 6)], wx[n4 % 2]).then_inc(bn_ok, 1)
                if live(base, n1):
                    mean_var("2", LN_EPS, base, n1)
                if live(base, n0):
                    wait(dve, t0_ok, base + n0 + 1)
                    wait(dve, u_ok, base + n0)
                    sums("1", t0, base, n0)
                    mean_var("1", LN_EPS, base, n0)
                if live(base, n1):
                    wait(dve, rs_ok["2"], base + n1 + 1)
                    wait(dve, y2_tr, base + n1)
                    scale_tokens(y2, "2", p_t1).then_inc(y2_ok, 1)
                if live(base, n0):
                    wait(dve, rs_ok["1"], base + n0 + 1)
                    wait(dve, u_tr, base + n0)
                    for j in range(BLK):
                        s_ = dve.tensor_scalar(u[:, j * C:(j + 1) * C], t0[:, j * C:(j + 1) * C],
                                               mv["1"][:, 2 * j:2 * j + 1], rs["1"][:, j:j + 1],
                                               ALU.subtract, ALU.mult)
                    s_.then_inc(u_ok, 1)

            phase1(dve, step)

            dve.wait_ge(bn_ok, NT)
            dve.bn_aggr(bn_mv[:, :], bn_parts[:, :]).then_inc(bn_dve, 1)
            dve.wait_ge(bn_dve, 1)
            dve.tensor_scalar(bn_small[:, 0:1], bn_mv[:, 1:2], LN_EPS, None, ALU.add).then_inc(bn_dve, 1)
            dve.wait_ge(bn_pool, 1)
            dve.tensor_tensor(bn_scale[:, :], gamma, bn_small[:, 1:2], ALU.mult).then_inc(bn_dve, 1)
            dve.wait_ge(bn_dve, 3)
            dve.tensor_tensor(bn_small[:, 2:3], bn_mv[:, 0:1], bn_scale[:, :], ALU.mult).then_inc(bn_dve, 1)
            dve.wait_ge(bn_dve, 4)
            dve.tensor_tensor(bn_bias[:, :], beta, bn_small[:, 2:3], ALU.subtract).then_inc(bn_ready, 1)

            for b in range(B):
                buf = wx_buf[b % 2]
                done = b * (WARM - 1 + L)
                y_done = b * (WARM + L)

                def argument(g, s, count):
                    dve.wait_ge(z_mm[g], count)
                    dve.scalar_tensor_tensor(out=cols(pre[:, g * GC:(g + 1) * GC]), in0=group_of(buf, g, s),
                                             scalar=bn_scale[:, 0:1], in1=cols(banks[g][:, 0:GC]),
                                             op0=ALU.mult, op1=ALU.add).then_inc(pre_ok[g], 1)

                dve.wait_ge(bn_ready, 1)
                dve.wait_ge(wx_back[b % 2], 16 * (b // 2 + 1))
                with dve.Fori(1, WARM) as w:
                    for g in range(G):
                        argument(g, w + (L - WARM), w + done)
                for g in range(G):
                    dve.wait_ge(y_ok[g], y_done + WARM)
                dve.tensor_copy(start_y[:, 1:NC], warm_y[:, 0:NC - 1]).then_inc(start_ok, 1)
                dve.memset(start_y[:, 0:1], 0.0).then_inc(start_ok, 1)
                for g in range(G):
                    argument(g, 0, done + WARM)
                with dve.Fori(1, L) as s:
                    for g in range(G):
                        argument(g, s, s + done + WARM)
                for g in range(G):
                    dve.wait_ge(y_ok[g], y_done + WARM + L)
                dve.tensor_tensor(cols(diff[:, :]), by_step(buf)[:, :, L - 1, :], cols(warm_y[:, :]), ALU.subtract)\
                   .then_inc(checked_part, 1)
                dve.wait_ge(checked_part, 4 * b + 1)
                dve.tensor_tensor(diff[:, :], diff[:, :], diff[:, :], ALU.mult).then_inc(checked_part, 1)
                dve.wait_ge(checked_part, 4 * b + 2)
                dve.tensor_scalar(diff[:, :], diff[:, :], TOL * TOL, None, ALU.is_le).then_inc(checked_part, 1)
                dve.wait_ge(checked_part, 4 * b + 3)
                dve.tensor_reduce(agree[:, b:b + 1], diff[:, :], AX.X, ALU.min).then_inc(checked, 1)
                dve.wait_ge(checked, b + 1)
                dve.nop().then_inc(checked_part, 1)

            dve.tensor_reduce(agree_all[:, :], agree[:, :], AX.X, ALU.min).then_inc(checked, 1)
            dve.wait_ge(flag_mm, 1)
            dve.tensor_reduce(agree_f[:, :], banks[2][0:1, 0:C], AX.X, ALU.min).then_inc(flag_part, 1)
            dve.wait_ge(flag_part, 1)
            dve.tensor_copy(agree_i[:, :], agree_f[:, :]).then_inc(flag_ok, 1)

            dve.wait_ge(flag_ok, 1)
            ok = dve.alloc_register("dve_ok")
            dve.reg_load(ok, agree_i[0:1, 0:1])
            with dve.If_eq(ok, 0):
                dve.memset(seq_y_buf, 0.0).then_inc(seq_zero, 1)
                with dve.Fori(0, TPB) as t:
                    with dve.Fori(0, CPT) as c:
                        with dve.Fori(0, L) as s:
                            k = t * N + c * L + s
                            dve.wait_ge(seq_in, (t + 1) * 32)
                            dve.wait_ge(seq_z, k + 1)
                            dve.scalar_tensor_tensor(out=seq_pre_buf, in0=seq_wx[:, :, bass.ds(s * CPT + c, 1)]
                                                     .rearrange("p b o -> p (b o)"),
                                                     scalar=bn_scale[:, 0:1], in1=banks[3][:, 0:B],
                                                     op0=ALU.mult, op1=ALU.add).then_inc(seq_pre, 1)
                            dve.wait_ge(seq_y, k + 1)
                            at = seq_xp[:, :, bass.ds(c * L + s, 1)].rearrange("p b o -> p (b o)")
                            dve.tensor_tensor(at, at, seq_y_buf, ALU.add).then_inc(seq_add, 1)
            with dve.Else():
                dve.nop()

        @block.scalar
        def _(act):
            act.wait_ge(dve_prep, 15)

            def step(base, m):
                n0, n1, n2, n3, n4 = (m - k for k in range(5))

                def relus(blocks_):
                    for j in blocks_:
                        wait(act, hid_mm, 4 * (base + n2) + j + 1)
                        wait(act, hid_ok, 4 * (base + n2) - 3 + j)
                        act.activation(relu[j], (p_hb, p_t1, p_ha, p_hb)[j][:, :], ACT.Relu,
                                       bias=hid_bias[:, j:j + 1]).then_inc(relu_ok, 1)

                def squares(blocks_):
                    for j in blocks_:
                        wait(act, relu_ok, 4 * (base + n2) + j + 1)
                        wait(act, kva_mm if j < 2 else kv_mm, base + n2)
                        act.activation(hid[j], relu[j], ACT.Square).then_inc(hid_ok, 1)

                if live(base, n4):
                    wait(act, wx_mm, base + n4 + 1)
                    wait(act, wx_stored[n4 % 2], ring(base, n4 - 2, 2))
                    wait(act, bn_ok, base + n4 - 1)
                    act.activation(wx[n4 % 2].rearrange("p (s c) -> p c s", c=CPT),
                                   p_wx[:, :].rearrange("p (c s) -> p c s", s=L), ACT.Copy).then_inc(wx_ok, 1)
                if live(base, n1):
                    wait(act, t0_tr, base + n1 + 1)
                    wait(act, t1_ok, base + n1)
                    act.activation(t0_c, p_xp[:, :], ACT.Copy).then_inc(t0_c_ok, 1)
                    wait(act, u_tr, base + n1 + 1)
                    wait(act, gate_ok, base + n1)
                    act.activation(sg, p_u[:, :], ACT.Sigmoid, bias=b1, scale=g1).then_inc(sg_ok, 1)
                    act.activation(y1, p_u[:, :], ACT.Identity, bias=b1, scale=g1).then_inc(y1_ok, 1)
                if live(base, n2):
                    wait(act, rec_mm, base + n2 + 1)
                    wait(act, rkv_ok, base + n2 - 1)
                    act.activation(recep[n2 % 2], p_ha[:, :], ACT.Sigmoid, bias=hid_bias[:, HB:HB + 1])\
                       .then_inc(recep_ok, 1)
                    relus((0,))
                if live(base, n0):
                    wait(act, shift0_ok, base + n0 + 1)
                    wait(act, xg_ok, base + n0)
                    for j in range(BLK):
                        s_ = act.activation(xn[:, j * C:(j + 1) * C], p_x[:, j * C:(j + 1) * C], ACT.Identity,
                                            bias=shift0[:, j:j + 1], scale=rs["0"][:, j:j + 1])
                    s_.then_inc(xn_ok, 1)
                if live(base, n2):
                    relus((1,))
                    squares((0, 1))
                    relus((2, 3))
                    squares((2, 3))
                if live(base, n3):
                    wait(act, un_tr, base + n3 + 1)
                    wait(act, wx_mm, base + n3)
                    act.activation(un_c, p_xp[:, :], ACT.Copy).then_inc(un_c_ok, 1)
                if live(base, n1):
                    wait(act, y2_tr, base + n1 + 1)
                    wait(act, hid_mm, 4 * (base + n1))
                    act.activation(y2_hi[:, :], p_t1[:, :], ACT.Copy).then_inc(y2_hi_ok, 1)

            phase1(act, step)

            act.wait_ge(bn_ready, 1)
            for b in range(B):
                buf = wx_buf[b % 2]
                done = b * (WARM - 1 + L)

                def state(g, dst, count):
                    act.wait_ge(pre_ok[g], count)
                    act.activation(dst, cols(pre[:, g * GC:(g + 1) * GC]), ACT.Sigmoid, bias=bn_bias[:, 0:1])\
                       .then_inc(y_ok[g], 1)

                act.wait_ge(wx_back[b % 2], 16 * (b // 2 + 1))
                if b:
                    act.wait_ge(checked, b)
                for g in range(G):
                    act.activation(cols(warm_y[:, g * GC:(g + 1) * GC]), group_of(buf, g, L - WARM), ACT.Sigmoid,
                                   bias=bn_bias[:, 0:1], scale=bn_scale[:, 0:1]).then_inc(y_ok[g], 1)
                with act.Fori(1, WARM) as w:
                    for g in range(G):
                        state(g, cols(warm_y[:, g * GC:(g + 1) * GC]), w + done)
                for g in range(G):
                    state(g, group_of(buf, g, 0), done + WARM)
                with act.Fori(1, L) as s:
                    for g in range(G):
                        state(g, group_of(buf, g, s), s + done + WARM)

            act.wait_ge(flag_ok, 1)
            ok = act.alloc_register("act_ok")
            act.reg_load(ok, agree_i[0:1, 0:1])
            with act.If_eq(ok, 0):
                with act.Fori(0, T) as k:
                    act.wait_ge(seq_pre, k + 1)
                    act.activation(seq_y_buf, seq_pre_buf, ACT.Sigmoid, bias=bn_bias[:, 0:1]).then_inc(seq_y, 1)
            with act.Else():
                act.nop()

        @block.gpsimd
        def _(pool):
            pool.memset(ident[:, :], 0.0).then_inc(pool_prep, 1)
            pool.memset(neg_half[:, :], -0.5).then_inc(pool_prep, 1)
            pool.wait_ge(pool_prep, 2)
            pool.affine_select(out=ident[:, :], in_=ident[:, :], compare_op=ALU.not_equal, fill=1.0,
                               base=0, pattern=[[-1, C]], channel_multiplier=1).then_inc(pool_prep, 1)
            pool.wait_ge(dve_prep, 15)

            def inv_root(k, readers, base, n):
                wait(pool, var_ok[k], base + n + 1)
                for s_ in readers:
                    wait(pool, s_, base + n)
                pool.tensor_tensor(rs[k][:, :], veps[k][:, :], neg_half[:, :], ALU.pow).then_inc(rs_ok[k], 1)

            def step(base, m):
                n0, n1, n2, n3 = (m - k for k in range(4))
                if live(base, n3):
                    wait(pool, rkv_ok, base + n3 + 1)
                    wait(pool, xp_ok, base + n3)
                    pool.tensor_tensor(t2, rkv, t1[n3 % 4], ALU.add).then_inc(t2_ok, 1)
                if live(base, n0):
                    inv_root("0", (xn_ok,), base, n0)
                if live(base, n3):
                    inv_root("e", (un_ok,), base, n3)
                if live(base, n0):
                    wait(pool, xn_ok, base + n0 + 1)
                    wait(pool, t0_ok, base + n0)
                    pool.tensor_tensor(xg, xn, g0_row, ALU.mult).then_inc(xg_ok, 1)
                    wait(pool, xg_ok, base + n0 + 1)
                    wait(pool, t0_tr, base + n0)
                    wait(pool, u_ok, base + n0)
                    pool.tensor_tensor(t0, xg, b0_row, ALU.add).then_inc(t0_ok, 1)
                if live(base, n1):
                    inv_root("2", (y2_ok,), base, n1)
                if live(base, n0):
                    inv_root("1", (u_ok,), base, n0)

            phase1(pool, step)

            pool.wait_ge(bn_dve, 2)
            pool.tensor_tensor(bn_small[:, 1:2], bn_small[:, 0:1], neg_half[:, 0:1], ALU.pow).then_inc(bn_pool, 1)

            for b in range(B):
                for g in range(G):
                    pool.wait_ge(y_ok[g], (b + 1) * (WARM + L))
                for t in range(TPB):
                    k = (b * TPB + t) // 4
                    if t % 4 == 0:
                        pool.wait_ge(stage_in[k % 3], 16 * (k // 3 + 1))
                    at = stage[:, ((k % 3) * 4 + t % 4) * N:((k % 3) * 4 + t % 4 + 1) * N]\
                        .rearrange("p (c s) -> p c s", s=L)
                    pool.tensor_tensor(at, at, wx_buf[b % 2][:, t * N:(t + 1) * N]
                                       .rearrange("p (s c) -> p c s", c=CPT), ALU.add).then_inc(added, 1)


_INS = ['x', 'L0_conv_ln0_g', 'L0_conv_ln0_b', 'L0_conv_ln1_g', 'L0_conv_ln1_b', 'L0_conv_ln2_g',
        'L0_conv_ln2_b', 'L0_conv_W_out', 'L0_conv_W_whiten', 'L0_conv_W_key', 'L0_conv_W_recep',
        'L0_conv_W_value', 'L0_ffn_W', 'L0_ffn_V', 'L0_ffn_gamma', 'L0_ffn_beta']


def kernel(**inputs):
    import numpy as np
    import concourse.bacc as bacc
    from concourse.bass_utils import run_bass_kernel_spmd

    nc = bacc.Bacc("TRN2", target_bir_lowering=False, num_devices=1)
    arrays, args = {}, []
    for name in _INS:
        a = np.ascontiguousarray(inputs[name])
        arrays[f"in_{name}"] = a
        args.append(nc.dram_tensor(f"in_{name}", a.shape, mybir.dt.from_np(a.dtype), kind="ExternalInput").ap())
    out = nc.dram_tensor("out", arrays["in_x"].shape, mybir.dt.float32, kind="ExternalOutput")
    metaformer_kernel(nc, *args, out.ap())
    r = run_bass_kernel_spmd(nc, [arrays], core_ids=[0])
    return r.results[0]["out"]
```

```python
import concourse.bass as bass
from concourse import mybir
from contextlib import ExitStack


def metaformer_kernel(nc, x, ln0_g, ln0_b, ln1_g, ln1_b, ln2_g, ln2_b,
                      W_out, W_whiten, W_key, W_recep, W_value,
                      W_ffn, V_ffn, bn_gamma, bn_beta, out):
    f32, f32r, i32 = mybir.dt.float32, mybir.dt.float32r, mybir.dt.int32
    ALU, ACT, AX = mybir.AluOpType, mybir.ActivationFunctionType, mybir.AxisListType

    B, C, H, Wd = x.shape
    T = H * Wd
    N = 512
    NT = B * T // N
    TPB = T // N
    HB = W_key.shape[0] // C
    L = 16
    CPT = N // L
    NC = T // L
    BLK = N // C
    WARM = 14
    TOL = 2.0 ** -21
    G = 4
    GC = NC // G
    GT = TPB // G
    STAGE = 2
    STAGES = TPB // STAGE
    RING = 11
    EARLY = 7
    LN_EPS = 1e-5
    KAPPA = (1.0 + LN_EPS) ** -0.5
    EPS0 = LN_EPS * 1e-6 / (1.0 + LN_EPS)

    x_d = x.rearrange("b c h w -> b c (h w)")
    out_d = out.rearrange("b c h w -> b c (h w)")
    xp_d = nc.dram_tensor("x_prime", (C, NT * N), f32, kind="Internal").ap()
    wx_d = nc.dram_tensor("w_x", (C, NT * N), f32, kind="Internal").ap()

    ctx = ExitStack()
    with ctx:
        def sb(name, cols, dt=f32, rows=C):
            return ctx.enter_context(nc.sbuf_tensor(name, [rows, cols], dt))

        def sem(name):
            return ctx.enter_context(nc.semaphore(name))

        def sems(name, n):
            return [sem(f"{name}{i}") for i in range(n)]

        ident = sb("ident", C)
        center = sb("center", C)
        neg_half = sb("neg_half", BLK)
        vecs = sb("vecs", 6)
        g1, b1, g2, b2, gamma, beta = (vecs[:, k:k + 1] for k in range(6))
        assert 2 * N == NC
        ln0_rows = sb("ln0_rows", 2 * N)
        g0_row, b0_row = ln0_rows[:, 0:N], ln0_rows[:, N:2 * N]
        hid_bias = sb("hid_bias", HB + 1)
        key_hi, key_lo = sb("key_hi", HB * C, f32r), sb("key_lo", HB * C, f32r)
        rec_hi, rec_lo = sb("rec_hi", C, f32r), sb("rec_lo", C, f32r)
        wf_T = sb("wf_T", C)
        value_T = sb("value_T", HB * C)
        small_T = sb("small_T", 4 * C)
        out_T, rec_T, ffn_T, V_T = (small_T[:, k * C:(k + 1) * C] for k in range(4))

        y2_hi, y2_lo = sb("y2_hi", N, f32r), sb("y2_lo", N, f32r)

        wx_even = sb("wx_even", T)
        arena = sb("arena", (T // N + RING * STAGE) * N)
        wx_buf = [wx_even[:, :], arena[:, 0:T]]
        arena_at = [0]

        def tile(n=1):
            at = arena_at[0]
            arena_at[0] += n
            return [arena[:, (at + k) * N:(at + k + 1) * N] for k in range(n)]

        x_in = tile(8)
        (xn,), (xg,), (u,) = (tile() for _ in range(3))
        t0, t1 = tile(2), tile(2)
        (sg,), (y1,), (gate,), (y2,) = (tile() for _ in range(4))
        xt = tile(4)
        relu = tile(HB)
        hid = tile(HB)
        recep = tile(2)
        (rkv,) = tile()
        xp = tile(2)
        (wn,) = tile()
        wx = tile(2)
        assert arena_at[0] <= TPB + (RING - EARLY) * STAGE

        last_xp, last_y = wx_buf[(B - 2) % 2], wx_buf[(B - 1) % 2]
        LNS = ("0", "1", "2", "e")
        st = {k: sb(f"st{k}", BLK * 6) for k in LNS}
        mv = {k: sb(f"mv{k}", BLK * 2) for k in LNS}
        veps = {k: sb(f"veps{k}", BLK) for k in LNS}
        rs = {k: sb(f"rs{k}", BLK) for k in LNS}
        shift0 = sb("shift0", BLK)

        bn_parts = sb("bn_parts", NT * 6)
        bn_mv = sb("bn_mv", 2)
        bn_small = sb("bn_small", 3)
        bn_scale = sb("bn_scale", 1)
        bn_bias = sb("bn_bias", 1)
        zero_warm_y = [sb(f"warm_y{k}", 1 + NC) for k in range(2)]
        warm_y, first_y = [z[:, 1:1 + NC] for z in zero_warm_y], [z[:, 0:NC] for z in zero_warm_y]
        pre = sb("pre", NC)
        diff = ln0_rows
        agree = sb("agree", B)
        agree_all = sb("agree_all", 1)
        agree_f = sb("agree_f", 1, rows=1)
        agree_i = sb("agree_i", 1, i32, rows=1)

        banks = [ctx.enter_context(nc.psum_tensor(f"bank{k}", [C, N], f32)) for k in range(8)]
        p_x, p_u, p_xp, p_wx, p_ha, p_hb, p_y2, p_kv = banks
        p_hid = (p_hb, p_ha, p_y2, p_hb)

        rows_in, weights_in, pool_prep, dve_prep, pe_prep = (sem(n) for n in ("rows_in", "weights_in", "pool_prep", "dve_prep", "pe_prep"))
        x_loaded = sems("x_loaded", 8)
        xp_stored = sems("xp_stored", 2)
        wx_stored = sems("wx_stored", 2)
        var_ok = {k: sem(f"var{k}_ok") for k in LNS}
        mv_part = {k: sem(f"mv{k}_part") for k in LNS}
        aggr_turn = sem("aggr_turn")
        shift0_ok, u_ok, y2_ok, wn_ok, y2_lo_ok, rkv_ok, t1_ok, xt_ok, bn_ok = (
            sem(n) for n in ("shift0_ok", "u_ok", "y2_ok", "wn_ok", "y2_lo_ok", "rkv_ok", "t1_ok", "xt_ok", "bn_ok"))
        rs_ok = {k: sem(f"rs{k}_ok") for k in LNS}
        xg_ok, t0_ok, gate_ok, xp_ok = (sem(n) for n in ("xg_ok", "t0_ok", "gate_ok", "xp_ok"))
        hid_ok, sg_ok, y1_ok, xn_ok, y2_hi_ok, recep_ok, relu_ok, wx_ok = (
            sem(n) for n in ("hid_ok", "sg_ok", "y1_ok", "xn_ok", "y2_hi_ok", "recep_ok", "relu_ok", "wx_ok"))
        x_tr, t1_tr, xp_tr, u_tr, y2_tr, wn_tr = (
            sem(n) for n in ("x_tr", "t1_tr", "xp_tr", "u_tr", "y2_tr", "wn_tr"))
        att_mm, rec_mm, hid_mm, kva_mm, kv_mm, wx_mm = (
            sem(n) for n in ("att_mm", "rec_mm", "hid_mm", "kva_mm", "kv_mm", "wx_mm"))
        bn_dve, bn_pool, bn_ready = sem("bn_dve"), sem("bn_pool"), sem("bn_ready")
        wx_back = sems("wx_back", 2)
        stage_in = sems("stage_in", RING)
        stage_out = sems("stage_out", RING)
        z_mm, pre_ok, y_ok = sems("z_mm", G), sems("pre_ok", G), sems("y_ok", G)
        added, added_step, checked, checked_part, agreed, flag_mm, flag_part, flag_ok = (
            sem(n) for n in ("added", "added_step", "checked", "checked_part", "agreed", "flag_mm", "flag_part", "flag_ok"))
        last_xp_in, last_dve, last_pool, last_out = (
            sem(n) for n in ("last_xp_in", "last_dve", "last_pool", "last_out"))
        seq_in, seq_out, seq_free, seq_z, seq_pre, seq_y, seq_add, seq_zero = (
            sem(n) for n in ("seq_in", "seq_out", "seq_free", "seq_z", "seq_pre", "seq_y", "seq_add", "seq_zero"))

        PREP_DMAS = 6 + 7

        LAG = 7
        FIRST = LAG + 3
        LOOP_END = (NT - FIRST) // 8 * 8

        def phase1(eng, step):
            for i in range(1, FIRST):
                step(0, i)
            with eng.Fori(0, LOOP_END - 7, 8) as base:
                for m in range(FIRST, FIRST + 8):
                    step(base, m)
            for i in range(FIRST + LOOP_END, NT + LAG):
                step(0, i)

        def live(base, n):
            return not isinstance(base, int) or 0 <= base + n < NT

        def wait(eng, s, count):
            if not isinstance(count, int) or count > 0:
                eng.wait_ge(s, count)

        def ring(base, m, size, each=16):
            return base * (each // size) + each * (m // size + 1)

        seq_wx = wx_even[:, 0:B * N].rearrange("c (b n) -> c b n", b=B)
        seq_xp = wx_even[:, B * N:2 * B * N].rearrange("c (b n) -> c b n", b=B)
        seq_y_buf = diff[:, 0:B]
        seq_pre_buf = pre[:, 0:B]

        def blocks(ap):
            return ap.rearrange("p (j c) -> p j c", c=C)

        def by_block(buf):
            return buf[:, :].rearrange("p (j k) -> p j k", j=BLK)

        def per_token(ap):
            return ap.unsqueeze(2).to_broadcast([C, BLK, C])

        def by_step(buf):
            return buf.rearrange("p (t s c) -> p t s c", s=L, c=CPT)

        def group_of(buf, g, s):
            return by_step(buf)[:, g * GT:(g + 1) * GT, bass.ds(s, 1), :].rearrange("p t s c -> p (t s) c")

        def wx_in(b):
            return 16 * ((TPB, 1)[b % 2] + STAGES * (b // 2))

        def stage(k):
            at = TPB + (k + RING - EARLY) % RING * STAGE
            return arena[:, at * N:(at + STAGE) * N]

        def by_dve(t):
            return t % 4 != 3

        def add_last(eng, t, done):
            at = last_xp[:, t * N:(t + 1) * N].rearrange("p (c s) -> p c s", s=L)
            eng.tensor_tensor(at, at, last_y[:, t * N:(t + 1) * N].rearrange("p (s c) -> p c s", c=CPT), ALU.add)\
               .then_inc(done, 1)

        def cols(ap):
            return ap.rearrange("p (t c) -> p t c", c=CPT)

        block = ctx.enter_context(nc.Block())

        @block.sync
        def _(sp):
            SW = STAGE * N

            def stage_load(k):
                if k >= RING:
                    sp.wait_ge(stage_out[k % RING], 16 * (k // RING))
                sp.dma_start(stage(k), xp_d[:, k * SW:(k + 1) * SW]).then_inc(stage_in[k % RING], 16)

            def load_and_store(b, base, m):
                if live(base, m - 8):
                    wait(sp, xt_ok, base + m - 7)
                if live(base, m):
                    col = (base + m - b * TPB) * N
                    sp.dma_start(x_in[m % 8], x_d[b, :, bass.ds(col, N)]).then_inc(x_loaded[m % 8], 16)
                if live(base, m - 10):
                    wait(sp, xp_ok, base + m - 9)
                    sp.dma_start(xp_d[:, bass.ds((base + m - 10) * N, N)], xp[m % 2]).then_inc(xp_stored[m % 2], 16)
                if live(base, m - 12):
                    wait(sp, wx_ok, base + m - 11)
                    sp.dma_start(wx_d[:, bass.ds((base + m - 12) * N, N)], wx[m % 2])\
                      .then_inc(wx_stored[m % 2], 16)

            load_and_store(0, 0, 0)
            for k, v in enumerate((ln0_g, ln0_b)):
                sp.dma_start(blocks(ln0_rows[:, k * N:(k + 1) * N]),
                             v.partition_broadcast(C).unsqueeze(1).to_broadcast([C, BLK, C])).then_inc(rows_in, 16)
            sp.dma_start(blocks(hid[0]), W_key.rearrange("(j p) c -> p j c", p=C)).then_inc(weights_in, 16)
            sp.dma_start(hid[1][:, :], W_value).then_inc(weights_in, 16)
            for k, w in enumerate((W_out, W_recep, W_ffn, V_ffn)):
                sp.dma_start(hid[2][:, k * C:(k + 1) * C], w).then_inc(weights_in, 16)
            sp.dma_start(hid[3][:, 0:C], W_whiten).then_inc(weights_in, 16)
            for m in range(1, 16):
                load_and_store(0, 0, m)
            for b in range(B):
                if b == 3:
                    for s in xp_stored:
                        sp.wait_ge(s, 16 * TPB // 2)
                    for k in range(EARLY):
                        stage_load(k)
                if b == 2:
                    for s in wx_stored:
                        sp.wait_ge(s, 16 * TPB // 2)
                with sp.Fori(max(b * TPB, 16), (b + 1) * TPB - 7, 8) as base:
                    for m in range(8):
                        load_and_store(b, base, m)
                        if b == 2:
                            sp.dma_start(wx_buf[0][:, bass.ds((base + m - b * TPB) * N, N)],
                                         wx_d[:, bass.ds((base + m - b * TPB) * N, N)]).then_inc(wx_back[0], 16)
            for m in range(NT, NT + 12):
                load_and_store(B - 1, 0, m)

            for s in xp_stored + wx_stored:
                sp.wait_ge(s, 16 * NT // 2)
            sp.wait_ge(bn_ok, NT)
            sp.dma_start(wx_buf[1], wx_d[:, T:2 * T]).then_inc(wx_back[1], 16)
            for k in range(EARLY, RING):
                stage_load(k)
            for b in range(B - 1):
                for j in range(STAGES):
                    k, at = b * STAGES + j, j * SW
                    sp.wait_ge(added, STAGE * (k + 1))
                    sp.dma_start(out_d[b, :, at:at + SW], stage(k)).then_inc(stage_out[k % RING], 16)
                    if j == 0:
                        sp.wait_ge(checked_part, 2 * b + 1)
                    free = wx_buf[b % 2][:, at:at + SW]
                    if b + 2 < B:
                        sp.dma_start(free, wx_d[:, (b + 2) * T + at:(b + 2) * T + at + SW]).then_inc(wx_back[b % 2], 16)
                    else:
                        sp.dma_start(free, xp_d[:, (b + 1) * T + at:(b + 1) * T + at + SW]).then_inc(last_xp_in, 16)
                    if j >= 2 and j - 2 + RING < STAGES:
                        stage_load(k - 2 + RING)
                if b + 2 < B:
                    for j in range(RING):
                        stage_load((b + 1) * STAGES + j)
            for k in range(STAGES):
                tiles = [by_dve(t) for t in range((k + 1) * STAGE)]
                sp.wait_ge(last_dve, sum(tiles))
                if len(tiles) > sum(tiles):
                    sp.wait_ge(last_pool, len(tiles) - sum(tiles))
                sp.dma_start(out_d[B - 1, :, k * SW:(k + 1) * SW], last_xp[:, k * SW:(k + 1) * SW])\
                  .then_inc(last_out, 16)
            for s in range(RING):
                sp.wait_ge(stage_out[s], 16 * (((B - 1) * STAGES - 1 - s) // RING + 1))
            sp.wait_ge(last_out, 16 * STAGES)

            sp.wait_ge(flag_ok, 1)
            ok = sp.alloc_register("sp_ok")
            sp.reg_load(ok, agree_i[0:1, 0:1])
            with sp.If_eq(ok, 0):
                with sp.Fori(0, TPB) as t:
                    for dst, src in ((seq_wx, wx_d), (seq_xp, xp_d)):
                        sp.dma_start(dst, src.rearrange("c (b n) -> c b n", b=B)[:, :, bass.ds(t * N, N)])\
                          .then_inc(seq_in, 16)
                    sp.wait_ge(seq_add, (t + 1) * N)
                    sp.dma_start(out_d.rearrange("b c n -> c b n")[:, :, bass.ds(t * N, N)], seq_xp)\
                      .then_inc(seq_out, 16)
                    sp.wait_ge(seq_out, (t + 1) * 16)
                    sp.sem_inc(seq_free, 1)
            with sp.Else():
                sp.nop()

        @block.tensor
        def _(pe):
            def turn(bank, tile):
                for j in range(BLK):
                    mm = pe.transpose(bank[:, j * C:(j + 1) * C], tile[:, j * C:(j + 1) * C], ident[:, :])
                return mm

            def mm3(bank, hi, lo, m_hi, m_lo):
                pe.matmul(bank, lo, m_hi, start=True, stop=False)
                pe.matmul(bank, hi, m_lo, start=False, stop=False)
                return pe.matmul(bank, hi, m_hi, start=False, stop=True)

            def mm_tokens(bank, tile, weights):
                for j in range(BLK):
                    mm = pe.matmul(bank[:, j * C:(j + 1) * C], tile[:, j * C:(j + 1) * C], weights,
                                   start=True, stop=True)
                return mm

            def step(base, m):
                n0, n1, n2, n3, n4, n5, n6 = (m - k for k in range(7))

                def hidden(j):
                    mm3(p_hid[j][:, :], key_hi[:, j * C:(j + 1) * C], key_lo[:, j * C:(j + 1) * C],
                        y2_hi[:, :], y2_lo[:, :]).then_inc(hid_mm, 1)

                def value(second):
                    for j in range(2 * second, 2 * second + 2):
                        wait(pe, hid_ok, 4 * (base + n4) + j + 1)
                        mm = pe.matmul(p_kv[:, :], value_T[:, j * C:(j + 1) * C], hid[j],
                                       start=(j == 0), stop=(j == HB - 1))
                    mm.then_inc(kv_mm if second else kva_mm, 1)

                if live(base, n0):
                    wait(pe, x_loaded[n0 % 8], ring(base, n0, 8))
                    wait(pe, xn_ok, base + n0)
                    turn(p_x, x_in[n0 % 8]).then_inc(x_tr, 1)
                if live(base, n3):
                    wait(pe, y2_ok, base + n3 + 1)
                    wait(pe, relu_ok, 4 * (base + n3) - 1)
                    turn(p_y2, y2).then_inc(y2_tr, 1)
                if live(base, n2):
                    wait(pe, gate_ok, base + n2 + 1)
                    if not live(base, n1):
                        wait(pe, t1_ok, base + n2)
                    mm_tokens(p_u, gate, out_T).then_inc(att_mm, 1)
                if live(base, n4):
                    wait(pe, rkv_ok, base + n4)
                    value(0)
                if live(base, n5):
                    wait(pe, xp_ok, base + n5 + 1)
                    if live(base, n5 - 2):
                        wait(pe, wx_ok, base + n5 - 1)
                    else:
                        wait(pe, mv_part["e"], 2 * (base + n5) - 1)
                    turn(p_xp, xp[n5 % 2]).then_inc(xp_tr, 1)
                if live(base, n4):
                    value(1)
                if live(base, n3):
                    wait(pe, y2_hi_ok, base + n3 + 1)
                    wait(pe, y2_lo_ok, base + n3 + 1)
                    mm3(p_ha[:, :], rec_hi[:, :], rec_lo[:, :], y2_hi[:, :], y2_lo[:, :]).then_inc(rec_mm, 1)
                    wait(pe, relu_ok, 4 * (base + n3))
                    hidden(0)
                if live(base, n1):
                    wait(pe, u_ok, base + n1 + 1)
                    wait(pe, t1_ok, base + n1)
                    turn(p_u, u).then_inc(u_tr, 1)
                if live(base, n2):
                    wait(pe, t1_ok, base + n2 + 1)
                    if live(base, n6):
                        wait(pe, wn_ok, base + n6 + 1)
                    else:
                        wait(pe, xt_ok, base + n2)
                    turn(p_wx, t1[n2 % 2]).then_inc(t1_tr, 1)
                if live(base, n3):
                    wait(pe, recep_ok, base + n3 + 1)
                    hidden(1)
                    hidden(2)
                if live(base, n6):
                    wait(pe, wn_ok, base + n6 + 1)
                    if live(base, n5):
                        wait(pe, mv_part["e"], 2 * (base + n5) + 1)
                    else:
                        wait(pe, wx_ok, base + n6)
                    turn(p_xp, wn).then_inc(wn_tr, 1)
                if live(base, n3):
                    wait(pe, relu_ok, 4 * (base + n3) + 1)
                    hidden(3)
                if live(base, n5):
                    if live(base, n2):
                        wait(pe, xt_ok, base + n2 + 1)
                    mm_tokens(p_wx, xp[n5 % 2], wf_T[:, :]).then_inc(wx_mm, 1)

            pe.wait_ge(pool_prep, 5)
            step(0, 0)

            pe.wait_ge(weights_in, 16 * PREP_DMAS)
            pe.wait_ge(xn_ok, 1)
            for j in range(HB):
                pe.transpose(p_x[:, j * C:(j + 1) * C], hid[0][:, j * C:(j + 1) * C], ident[:, :])
                pe.transpose(p_y2[:, j * C:(j + 1) * C], hid[1][:, j * C:(j + 1) * C], ident[:, :])
                mm = pe.transpose(p_xp[:, j * C:(j + 1) * C], hid[2][:, j * C:(j + 1) * C], ident[:, :])
            mm.then_inc(pe_prep, 1)
            pe.wait_ge(dve_prep, 5)
            pe.matmul(p_u[:, 0:C], center[:, :], ffn_T, start=True, stop=True)
            pe.matmul(p_ha[:, :], hid[3][:, 0:C], sg, start=True, stop=True)
            pe.matmul(p_hb[:, 0:C], hid[3][:, 0:C], rec_T, start=True, stop=True).then_inc(pe_prep, 1)
            pe.wait_ge(dve_prep, 10)
            for j in range(HB):
                pe.matmul(p_kv[:, j:j + 1], y1[:, j * C:(j + 1) * C], b2, start=True, stop=True)
            pe.matmul(p_kv[:, HB:HB + 1], gate[:, 0:C], b2, start=True, stop=True)
            pe.matmul(p_x[:, :], center[:, :], y2, start=True, stop=True)
            pe.matmul(p_y2[:, 0:C], center[:, :], u[:, 0:C], start=True, stop=True).then_inc(pe_prep, 1)
            pe.wait_ge(dve_prep, 15)
            phase1(pe, step)

            def v_y(g, y):
                pe.matmul(banks[g][:, 0:GC], V_T, y, start=True, stop=True).then_inc(z_mm[g], 1)

            pe.wait_ge(bn_ok, NT)
            for b in range(B):
                done = b * (WARM + L)
                with pe.Fori(1, WARM) as w:
                    for g in range(G):
                        pe.wait_ge(y_ok[g], w + done)
                        v_y(g, warm_y[b % 2][:, g * GC:(g + 1) * GC])
                for g in range(G):
                    pe.wait_ge(y_ok[g], done + WARM)
                    v_y(g, first_y[b % 2][:, g * GC:(g + 1) * GC])
                with pe.Fori(1, L) as s:
                    for g in range(G):
                        pe.wait_ge(y_ok[g], s + done + WARM)
                        v_y(g, group_of(wx_buf[b % 2], g, s - 1))

            pe.wait_ge(agreed, B + 1)
            pe.transpose(banks[2][0:1, 0:C], agree_all[:, :], ident[:, :]).then_inc(flag_mm, 1)

            pe.wait_ge(flag_ok, 1)
            ok = pe.alloc_register("pe_ok")
            pe.reg_load(ok, agree_i[0:1, 0:1])
            with pe.If_eq(ok, 0):
                pe.wait_ge(seq_zero, 1)
                pe.matmul(banks[3][:, 0:B], V_T, seq_y_buf, start=True, stop=True).then_inc(seq_z, 1)
                with pe.Fori(1, T) as k:
                    pe.wait_ge(seq_y, k)
                    pe.matmul(banks[3][:, 0:B], V_T, seq_y_buf, start=True, stop=True).then_inc(seq_z, 1)
            with pe.Else():
                pe.nop()

        @block.vector
        def _(dve):
            def sums(k, tile, base, n):
                wait(dve, mv_part[k], 2 * (base + n))
                for j in range(BLK):
                    s_ = dve.bn_stats(st[k][:, 6 * j:6 * j + 6], tile[:, j * C:(j + 1) * C])
                s_.then_inc(mv_part[k], 1)

            def mean_var(k, base, n):
                wait(dve, mv_part[k], 2 * (base + n) + 1)
                wait(dve, var_ok[k], base + n)
                dve.sem_inc(aggr_turn, 1)
                for j in range(BLK):
                    s_ = dve.bn_aggr(mv[k][:, 2 * j:2 * j + 2], st[k][:, 6 * j:6 * j + 6])
                s_.then_inc(mv_part[k], 1)

            def add_eps(k, eps, base, n):
                wait(dve, mv_part[k], 2 * (base + n) + 2)
                wait(dve, rs_ok[k], base + n)
                dve.tensor_scalar(veps[k][:, :], by_block(mv[k])[:, :, 1], eps, None, ALU.add).then_inc(var_ok[k], 1)

            def scale_tokens(dst, k, src):
                return dve.tensor_tensor(blocks(dst), blocks(src), per_token(rs[k][:, :]), ALU.mult)

            def step(base, m):
                n0, n1, n2, n3, n4, n5, n6, n7 = (m - k for k in range(8))
                if live(base, n0):
                    wait(dve, x_tr, base + n0 + 1)
                    sums("0", p_x, base, n0)
                    wait(dve, shift0_ok, base + n0)
                    mean_var("0", base, n0)
                    add_eps("0", EPS0, base, n0)
                if live(base, n2):
                    wait(dve, att_mm, base + n2 + 1)
                    wait(dve, t1_tr, base + n2 - 1)
                    wait(dve, y2_ok, base + n2 - 1)
                    dve.tensor_tensor(t1[n2 % 2], p_u[:, :], t0[n2 % 2], ALU.add).then_inc(t1_ok, 1)
                if live(base, n6):
                    wait(dve, rs_ok["e"], base + n6 + 1)
                    wait(dve, wx_mm, base + n6 + 1)
                    wait(dve, wn_tr, base + n6)
                    scale_tokens(wn, "e", p_wx[:, :]).then_inc(wn_ok, 1)
                if live(base, n0):
                    wait(dve, rs_ok["0"], base + n0 + 1)
                    wait(dve, xn_ok, base + n0)
                    dve.scalar_tensor_tensor(out=shift0[:, :], in0=by_block(mv["0"])[:, :, 0], scalar=-1.0,
                                             in1=rs["0"][:, :], op0=ALU.mult, op1=ALU.mult).then_inc(shift0_ok, 1)
                if live(base, n2):
                    wait(dve, t1_ok, base + n2 + 1)
                    sums("2", t1[n2 % 2], base, n2)
                if live(base, n3):
                    wait(dve, y2_hi_ok, base + n3 + 1)
                    wait(dve, hid_mm, 4 * (base + n3))
                    dve.tensor_tensor(y2_lo[:, :], p_y2[:, :], y2_hi[:, :].bitcast(f32), ALU.subtract)\
                       .then_inc(y2_lo_ok, 1)
                if live(base, n2):
                    mean_var("2", base, n2)
                if live(base, n1):
                    wait(dve, rs_ok["1"], base + n1 + 1)
                    wait(dve, u_tr, base + n1)
                    for j in range(BLK):
                        s_ = dve.tensor_scalar(u[:, j * C:(j + 1) * C], t0[n1 % 2][:, j * C:(j + 1) * C],
                                               mv["1"][:, 2 * j:2 * j + 1], rs["1"][:, j:j + 1],
                                               ALU.subtract, ALU.mult)
                    s_.then_inc(u_ok, 1)
                if live(base, n5):
                    wait(dve, xp_tr, base + n5 + 1)
                    sums("e", p_xp, base, n5)
                if live(base, n4):
                    wait(dve, kv_mm, base + n4 + 1)
                    wait(dve, recep_ok, base + n4 + 1)
                    wait(dve, xp_ok, base + n4)
                    dve.tensor_tensor(rkv, p_kv[:, :], recep[n4 % 2], ALU.mult).then_inc(rkv_ok, 1)
                if live(base, n2):
                    add_eps("2", LN_EPS, base, n2)
                if live(base, n5):
                    mean_var("e", base, n5)
                if live(base, n2):
                    wait(dve, t1_tr, base + n2 + 1)
                    wait(dve, xp_ok, base + n2 - 3)
                    dve.scalar_tensor_tensor(out=xt[n2 % 4], in0=p_wx[:, :], scalar=2.0, in1=x_in[n2 % 8],
                                             op0=ALU.mult, op1=ALU.add).then_inc(xt_ok, 1)
                if live(base, n0):
                    wait(dve, t0_ok, base + n0 + 1)
                    sums("1", t0[n0 % 2], base, n0)
                if live(base, n7):
                    wait(dve, wx_ok, base + n7 + 1)
                    dve.bn_stats(bn_parts[:, bass.ds((base + n7) * 6, 6)], wx[n7 % 2]).then_inc(bn_ok, 1)
                if live(base, n5):
                    add_eps("e", LN_EPS, base, n5)
                if live(base, n2):
                    wait(dve, rs_ok["2"], base + n2 + 1)
                    wait(dve, y2_tr, base + n2)
                    scale_tokens(y2, "2", t1[n2 % 2]).then_inc(y2_ok, 1)
                if live(base, n0):
                    wait(dve, u_ok, base + n0)
                    mean_var("1", base, n0)
                    add_eps("1", LN_EPS, base, n0)

            dve.wait_ge(pool_prep, 5)
            dve.tensor_scalar(center[:, :], ident[:, :], -1.0 / C, None, ALU.add).then_inc(dve_prep, 1)
            dve.wait_ge(rows_in, 32)
            dve.tensor_scalar(g0_row, g0_row, KAPPA, None, ALU.mult).then_inc(dve_prep, 1)
            step(0, 0)

            dve.wait_ge(weights_in, 16 * PREP_DMAS)
            dve.wait_ge(pe_prep, 1)
            dve.tensor_copy(sg, p_x[:, :]).then_inc(dve_prep, 1)
            dve.tensor_scalar(value_T[:, :], p_y2[:, :], 2.0, None, ALU.mult).then_inc(dve_prep, 1)
            dve.tensor_copy(small_T[:, :], p_xp[:, :]).then_inc(dve_prep, 1)
            dve.wait_ge(pe_prep, 2)
            dve.tensor_copy(wf_T[:, :], p_u[:, 0:C]).then_inc(dve_prep, 1)
            dve.tensor_copy(y1, p_ha[:, :]).then_inc(dve_prep, 1)
            dve.tensor_copy(gate[:, 0:C], p_hb[:, 0:C]).then_inc(dve_prep, 1)
            dve.tensor_scalar(y2, p_ha[:, :], g2, None, ALU.mult).then_inc(dve_prep, 1)
            dve.tensor_scalar(u[:, 0:C], p_hb[:, 0:C], g2, None, ALU.mult).then_inc(dve_prep, 1)
            dve.wait_ge(pe_prep, 3)
            dve.tensor_copy(hid_bias[:, :], p_kv[:, 0:HB + 1]).then_inc(dve_prep, 1)
            dve.tensor_copy(key_hi[:, :], p_x[:, :]).then_inc(dve_prep, 1)
            dve.tensor_copy(rec_hi[:, :], p_y2[:, 0:C]).then_inc(dve_prep, 1)
            dve.wait_ge(dve_prep, 13)
            dve.tensor_tensor(key_lo[:, :], p_x[:, :], key_hi[:, :].bitcast(f32), ALU.subtract).then_inc(dve_prep, 1)
            dve.tensor_tensor(rec_lo[:, :], p_y2[:, 0:C], rec_hi[:, :].bitcast(f32), ALU.subtract).then_inc(dve_prep, 1)
            phase1(dve, step)

            dve.wait_ge(bn_ok, NT)
            dve.bn_aggr(bn_mv[:, :], bn_parts[:, :]).then_inc(bn_dve, 1)
            dve.wait_ge(bn_dve, 1)
            dve.tensor_scalar(bn_small[:, 0:1], bn_mv[:, 1:2], LN_EPS, None, ALU.add).then_inc(bn_dve, 1)
            dve.wait_ge(bn_pool, 1)
            dve.tensor_tensor(bn_scale[:, :], gamma, bn_small[:, 1:2], ALU.mult).then_inc(bn_dve, 1)
            dve.wait_ge(bn_dve, 3)
            dve.tensor_tensor(bn_small[:, 2:3], bn_mv[:, 0:1], bn_scale[:, :], ALU.mult).then_inc(bn_dve, 1)
            dve.wait_ge(bn_dve, 4)
            dve.tensor_tensor(bn_bias[:, :], beta, bn_small[:, 2:3], ALU.subtract).then_inc(bn_ready, 1)

            def all_agree(b):
                dve.wait_ge(checked, b + 1)
                dve.tensor_reduce(agree[:, b:b + 1], diff[:, :], AX.X, ALU.min).then_inc(agreed, 1)

            for b in range(B):
                buf = wx_buf[b % 2]
                done = b * (WARM - 1 + L)

                def argument(g, s, count):
                    dve.wait_ge(z_mm[g], count)
                    dve.scalar_tensor_tensor(out=cols(pre[:, g * GC:(g + 1) * GC]), in0=group_of(buf, g, s),
                                             scalar=bn_scale[:, 0:1], in1=cols(banks[g][:, 0:GC]),
                                             op0=ALU.mult, op1=ALU.add).then_inc(pre_ok[g], 1)

                dve.wait_ge(bn_ready, 1)
                dve.wait_ge(wx_back[b % 2], wx_in(b))
                with dve.Fori(1, WARM) as w:
                    for g in range(G):
                        argument(g, w + (L - WARM), w + done)
                for g in range(G):
                    argument(g, 0, done + WARM)
                with dve.Fori(1, L) as s:
                    for g in range(G):
                        argument(g, s, s + done + WARM)
                if b:
                    all_agree(b - 1)

            for g in range(G):
                dve.wait_ge(y_ok[g], B * (WARM + L))
            dve.wait_ge(last_xp_in, 16 * STAGES)
            for t in range(TPB):
                if by_dve(t):
                    add_last(dve, t, last_dve)
            all_agree(B - 1)
            dve.wait_ge(agreed, B)
            dve.tensor_reduce(agree_all[:, :], agree[:, :], AX.X, ALU.min).then_inc(agreed, 1)
            dve.wait_ge(flag_mm, 1)
            dve.tensor_reduce(agree_f[:, :], banks[2][0:1, 0:C], AX.X, ALU.min).then_inc(flag_part, 1)
            dve.wait_ge(flag_part, 1)
            dve.tensor_copy(agree_i[:, :], agree_f[:, :]).then_inc(flag_ok, 1)

            dve.wait_ge(flag_ok, 1)
            ok = dve.alloc_register("dve_ok")
            dve.reg_load(ok, agree_i[0:1, 0:1])
            with dve.If_eq(ok, 0):
                dve.memset(seq_y_buf, 0.0).then_inc(seq_zero, 1)
                with dve.Fori(0, TPB) as t:
                    with dve.Fori(0, CPT) as c:
                        with dve.Fori(0, L) as s:
                            k = t * N + c * L + s
                            dve.wait_ge(seq_in, (t + 1) * 32)
                            dve.wait_ge(seq_z, k + 1)
                            dve.scalar_tensor_tensor(out=seq_pre_buf, in0=seq_wx[:, :, bass.ds(s * CPT + c, 1)]
                                                     .rearrange("p b o -> p (b o)"),
                                                     scalar=bn_scale[:, 0:1], in1=banks[3][:, 0:B],
                                                     op0=ALU.mult, op1=ALU.add).then_inc(seq_pre, 1)
                            dve.wait_ge(seq_y, k + 1)
                            at = seq_xp[:, :, bass.ds(c * L + s, 1)].rearrange("p b o -> p (b o)")
                            dve.tensor_tensor(at, at, seq_y_buf, ALU.add).then_inc(seq_add, 1)
            with dve.Else():
                dve.nop()

        @block.scalar
        def _(act):
            for k, v in enumerate((ln1_g, ln1_b, ln2_g, ln2_b, bn_gamma, bn_beta)):
                act.dma_start(vecs[:, k:k + 1], v.rearrange("(c o) -> c o", o=1)).then_inc(weights_in, 16)

            def step(base, m):
                n0, n1, _, n3, _, _, n6 = (m - k for k in range(7))

                def relus(blocks_):
                    for j in blocks_:
                        wait(act, hid_mm, 4 * (base + n3) + j + 1)
                        wait(act, hid_ok, 4 * (base + n3) - 3 + j)
                        act.activation(relu[j], p_hid[j][:, :], ACT.Relu,
                                       bias=hid_bias[:, j:j + 1]).then_inc(relu_ok, 1)

                def squares(blocks_):
                    for j in blocks_:
                        wait(act, relu_ok, 4 * (base + n3) + j + 1)
                        wait(act, kva_mm if j < 2 else kv_mm, base + n3)
                        act.activation(hid[j], relu[j], ACT.Square).then_inc(hid_ok, 1)

                if live(base, n3):
                    wait(act, y2_tr, base + n3 + 1)
                    wait(act, hid_mm, 4 * (base + n3))
                    act.activation(y2_hi[:, :], p_y2[:, :], ACT.Copy).then_inc(y2_hi_ok, 1)
                if live(base, n0):
                    wait(act, shift0_ok, base + n0 + 1)
                    wait(act, xg_ok, base + n0)
                    for j in range(BLK):
                        s_ = act.activation(xn[:, j * C:(j + 1) * C], p_x[:, j * C:(j + 1) * C], ACT.Identity,
                                            bias=shift0[:, j:j + 1], scale=rs["0"][:, j:j + 1])
                    s_.then_inc(xn_ok, 1)
                if live(base, n3):
                    wait(act, rec_mm, base + n3 + 1)
                    wait(act, rkv_ok, base + n3 - 1)
                    act.activation(recep[n3 % 2], p_ha[:, :], ACT.Sigmoid, bias=hid_bias[:, HB:HB + 1])\
                       .then_inc(recep_ok, 1)
                    relus((0,))
                if live(base, n1):
                    wait(act, u_tr, base + n1 + 1)
                    wait(act, gate_ok, base + n1)
                    act.activation(sg, p_u[:, :], ACT.Sigmoid, bias=b1, scale=g1).then_inc(sg_ok, 1)
                    act.activation(y1, p_u[:, :], ACT.Identity, bias=b1, scale=g1).then_inc(y1_ok, 1)
                if live(base, n3):
                    relus((1, 2))
                if live(base, n6):
                    wait(act, wn_tr, base + n6 + 1)
                    wait(act, wx_stored[n6 % 2], ring(base, n6 - 2, 2))
                    wait(act, bn_ok, base + n6 - 1)
                    act.activation(wx[n6 % 2].rearrange("p (s c) -> p c s", c=CPT),
                                   p_xp[:, :].rearrange("p (c s) -> p c s", s=L), ACT.Copy).then_inc(wx_ok, 1)
                if live(base, n3):
                    squares((0, 1, 2))
                    relus((3,))
                    squares((3,))

            step(0, 0)
            act.wait_ge(dve_prep, 15)
            phase1(act, step)

            act.wait_ge(bn_ready, 1)
            for b in range(B):
                buf = wx_buf[b % 2]
                done = b * (WARM - 1 + L)

                def state(g, dst, count):
                    act.wait_ge(pre_ok[g], count)
                    act.activation(dst, cols(pre[:, g * GC:(g + 1) * GC]), ACT.Sigmoid, bias=bn_bias[:, 0:1])\
                       .then_inc(y_ok[g], 1)

                act.wait_ge(wx_back[b % 2], wx_in(b))
                if b > 1:
                    act.wait_ge(checked, b - 1)
                for g in range(G):
                    act.activation(cols(warm_y[b % 2][:, g * GC:(g + 1) * GC]), group_of(buf, g, L - WARM), ACT.Sigmoid,
                                   bias=bn_bias[:, 0:1], scale=bn_scale[:, 0:1]).then_inc(y_ok[g], 1)
                with act.Fori(1, WARM) as w:
                    for g in range(G):
                        state(g, cols(warm_y[b % 2][:, g * GC:(g + 1) * GC]), w + done)
                for g in range(G):
                    state(g, group_of(buf, g, 0), done + WARM)
                with act.Fori(1, L) as s:
                    for g in range(G):
                        state(g, group_of(buf, g, s), s + done + WARM)

            act.wait_ge(flag_ok, 1)
            ok = act.alloc_register("act_ok")
            act.reg_load(ok, agree_i[0:1, 0:1])
            with act.If_eq(ok, 0):
                with act.Fori(0, T) as k:
                    act.wait_ge(seq_pre, k + 1)
                    act.activation(seq_y_buf, seq_pre_buf, ACT.Sigmoid, bias=bn_bias[:, 0:1]).then_inc(seq_y, 1)
            with act.Else():
                act.nop()

        @block.gpsimd
        def _(pool):
            pool.memset(ident[:, :], 0.0).then_inc(pool_prep, 1)
            pool.memset(neg_half[:, :], -0.5).then_inc(pool_prep, 1)
            for z in zero_warm_y:
                pool.memset(z[:, 0:1], 0.0).then_inc(pool_prep, 1)
            pool.wait_ge(pool_prep, 4)
            pool.affine_select(out=ident[:, :], in_=ident[:, :], compare_op=ALU.not_equal, fill=1.0,
                               base=0, pattern=[[-1, C]], channel_multiplier=1).then_inc(pool_prep, 1)

            def inv_root(k, readers, base, n):
                wait(pool, var_ok[k], base + n + 1)
                for s_ in readers:
                    wait(pool, s_, base + n)
                pool.tensor_tensor(rs[k][:, :], veps[k][:, :], neg_half[:, :], ALU.pow).then_inc(rs_ok[k], 1)

            def step(base, m):
                n0, n1, n2, _, n4, n5 = (m - k for k in range(6))
                if live(base, n0):
                    inv_root("0", (xn_ok,), base, n0)
                if live(base, n1):
                    inv_root("1", (u_ok,), base, n1)
                if live(base, n0):
                    wait(pool, xn_ok, base + n0 + 1)
                    wait(pool, t0_ok, base + n0)
                    pool.tensor_tensor(xg, xn, g0_row, ALU.mult).then_inc(xg_ok, 1)
                    wait(pool, xg_ok, base + n0 + 1)
                    wait(pool, t1_ok, base + n0 - 1)
                    wait(pool, u_ok, base + n0 - 1)
                    pool.tensor_tensor(t0[n0 % 2], xg, b0_row, ALU.add).then_inc(t0_ok, 1)
                if live(base, n4):
                    wait(pool, rkv_ok, base + n4 + 1)
                    wait(pool, xt_ok, base + n4 + 1)
                    wait(pool, xp_stored[n4 % 2], ring(base, n4 - 2, 2))
                    wait(pool, wx_mm, base + n4 - 1)
                    pool.tensor_tensor(xp[n4 % 2], rkv, xt[n4 % 4], ALU.add).then_inc(xp_ok, 1)
                if live(base, n2):
                    inv_root("2", (y2_ok,), base, n2)
                if live(base, n1):
                    wait(pool, sg_ok, base + n1 + 1)
                    wait(pool, y1_ok, base + n1 + 1)
                    wait(pool, att_mm, base + n1)
                    pool.tensor_tensor(gate, y1, sg, ALU.mult).then_inc(gate_ok, 1)
                if live(base, n5):
                    inv_root("e", (wn_ok,), base, n5)

            pool.wait_ge(dve_prep, 2)
            step(0, 0)
            pool.wait_ge(dve_prep, 15)
            phase1(pool, step)

            pool.wait_ge(bn_dve, 2)
            pool.tensor_tensor(bn_small[:, 1:2], bn_small[:, 0:1], neg_half[:, 0:1], ALU.pow).then_inc(bn_pool, 1)

            def compare(b):
                if b:
                    pool.wait_ge(agreed, b)
                pool.tensor_tensor(cols(diff[:, :]), by_step(wx_buf[b % 2])[:, :, L - 1, :], cols(warm_y[b % 2]),
                                   ALU.subtract).then_inc(checked_part, 1)

            def check(b):
                pool.wait_ge(checked_part, 2 * b + 1)
                pool.tensor_tensor(diff[:, :], diff[:, :], diff[:, :], ALU.mult).then_inc(checked_part, 1)
                pool.wait_ge(checked_part, 2 * b + 2)
                pool.tensor_scalar(diff[:, :], diff[:, :], TOL * TOL, None, ALU.is_le).then_inc(checked, 1)

            for k in range(RING):
                pool.wait_ge(stage_in[k], 16)
            with pool.Fori(0, L) as s:
                for tile_a, tile_b, place in ((0, EARLY * STAGE, RING - EARLY), (EARLY * STAGE, RING * STAGE, 0)):
                    for g in range((tile_b - 1) // GT + 1):
                        pool.wait_ge(y_ok[g], s + (WARM + 1))
                    first = (TPB + place * STAGE) * N
                    xp_ = arena[:, first:first + (tile_b - tile_a) * N].rearrange("p (q s) -> p q s", s=L)[:, :, bass.ds(s, 1)]\
                        .rearrange("p (t c) o -> p t (c o)", c=CPT)
                    y_ = by_step(wx_buf[0])[:, tile_a:tile_b, bass.ds(s, 1), :].rearrange("p t s c -> p t (s c)")
                    pool.tensor_tensor(xp_, xp_, y_, ALU.add).then_inc(added_step, 1)
            pool.wait_ge(added_step, 2 * L)
            pool.sem_inc(added, RING * STAGE)

            for b in range(B):
                for g in range(G):
                    pool.wait_ge(y_ok[g], (b + 1) * (WARM + L))
                if b < B - 1:
                    compare(b)
                    for t in range(0 if b else RING * STAGE, TPB):
                        k = (b * TPB + t) // STAGE
                        if t % STAGE == 0:
                            pool.wait_ge(stage_in[k % RING], 16 * (k // RING + 1))
                        xp_ = stage(k)[:, t % STAGE * N:(t % STAGE + 1) * N].rearrange("p (c s) -> p c s", s=L)
                        pool.tensor_tensor(xp_, xp_, wx_buf[b % 2][:, t * N:(t + 1) * N]
                                           .rearrange("p (s c) -> p c s", c=CPT), ALU.add).then_inc(added, 1)
                    check(b)
            pool.wait_ge(last_xp_in, 16 * STAGES)
            for t in range(TPB):
                if not by_dve(t):
                    add_last(pool, t, last_pool)
            compare(B - 1)
            check(B - 1)


_INS = ['x', 'L0_conv_ln0_g', 'L0_conv_ln0_b', 'L0_conv_ln1_g', 'L0_conv_ln1_b', 'L0_conv_ln2_g',
        'L0_conv_ln2_b', 'L0_conv_W_out', 'L0_conv_W_whiten', 'L0_conv_W_key', 'L0_conv_W_recep',
        'L0_conv_W_value', 'L0_ffn_W', 'L0_ffn_V', 'L0_ffn_gamma', 'L0_ffn_beta']


def kernel(**inputs):
    import numpy as np
    import concourse.bacc as bacc
    from concourse.bass_utils import run_bass_kernel_spmd

    nc = bacc.Bacc("TRN2", target_bir_lowering=False, num_devices=1)
    arrays, args = {}, []
    for name in _INS:
        a = np.ascontiguousarray(inputs[name])
        arrays[f"in_{name}"] = a
        args.append(nc.dram_tensor(f"in_{name}", a.shape, mybir.dt.from_np(a.dtype), kind="ExternalInput").ap())
    out = nc.dram_tensor("out", arrays["in_x"].shape, mybir.dt.float32, kind="ExternalOutput")
    metaformer_kernel(nc, *args, out.ap())
    r = run_bass_kernel_spmd(nc, [arrays], core_ids=[0])
    return r.results[0]["out"]
```
